# Optimizing a Trainium2 kernel written in Bass

```python
import numpy as np
import jax
import jax.numpy as jnp

def _softmax(x, axis=-1):
    return jax.nn.softmax(x, axis=axis)

def _gelu(x):
    return jax.nn.gelu(x, approximate=True)

def _silu(x):
    return jax.nn.silu(x)

def _sigmoid(x):
    return jax.nn.sigmoid(x)

def _layernorm(x, axis=-1, eps=1e-05):
    m = jnp.mean(x, axis=axis, keepdims=True)
    v = jnp.var(x, axis=axis, keepdims=True)
    return (x - m) / jnp.sqrt(v + eps)

def _scatter_add(tgt, idx, src, axis=0):
    return tgt.at[idx].add(src)

def _segment_sum(src, seg, n):
    return jax.ops.segment_sum(src, seg, n)
kernel_name = 'mk_early_fusion_d1_tok_img1024_r4_e8c935'

def setup_inputs(seed: int=0):
    np.random.seed(seed)
    _w = jnp.asarray

    def _rec_inputs():
        import jax
        import jax.numpy as jnp
        _rk = jax.random.key(seed)
        x = -0.00016672 + 0.999947 * jax.random.normal(jax.random.fold_in(_rk, 1), (32, 3, 64, 64), jnp.float32)
        txt = 0.435037 + 1.14557 * jax.random.normal(jax.random.fold_in(_rk, 2), (32, 32, 256), jnp.float32)
        return (x, txt)
    x, txt = _rec_inputs()

    def _L0_tok_setup():
        import jax, jax.numpy as jnp
        import numpy as np
        PATCH = 16
        EPS = 1e-05

        def _patchify(img, p):
            B, C, H, W = img.shape
            h, w = (H // p, W // p)
            x = img.reshape(B, C, h, p, w, p)
            x = x.transpose(0, 2, 4, 1, 3, 5)
            return x.reshape(B, h, w, C * p * p)

        def _layernorm(x, gamma):
            mu = x.mean(axis=-1, keepdims=True)
            var = ((x - mu) ** 2).mean(axis=-1, keepdims=True)
            return (x - mu) * jax.lax.rsqrt(var + EPS) * gamma

        def _posemb_sincos_2d(h, w, dim, temperature=10000.0, dtype=jnp.float32):
            y, x = jnp.meshgrid(jnp.arange(h, dtype=dtype), jnp.arange(w, dtype=dtype), indexing='ij')
            omega = jnp.arange(dim // 4, dtype=dtype) / (dim // 4 - 1)
            omega = 1.0 / temperature ** omega
            y = y.reshape(-1)[:, None] * omega[None, :]
            x = x.reshape(-1)[:, None] * omega[None, :]
            return jnp.concatenate([jnp.sin(x), jnp.cos(x), jnp.sin(y), jnp.cos(y)], axis=1)
        key = jax.random.key(seed)
        k1, k2, k3, k4 = jax.random.split(key, 4)
        patch_dim = 3 * PATCH * PATCH
        dim = 256
        img = jax.random.normal(k1, (64, 3, 96, 96), dtype=jnp.float32)
        ln1_w = jax.random.uniform(k2, (patch_dim,), dtype=jnp.float32, minval=0.9, maxval=1.1)
        W = jax.random.normal(k3, (dim, patch_dim), dtype=jnp.float32) * 0.02
        ln2_w = jax.random.uniform(k4, (dim,), dtype=jnp.float32, minval=0.9, maxval=1.1)
        return {'img': img, 'ln1_w': ln1_w, 'W': W, 'ln2_w': ln2_w}
    _L0_tok_all = _L0_tok_setup()
    _L0_tok_in = {k: v for k, v in _L0_tok_all.items() if k in ('ln1_w', 'W', 'ln2_w')}
    del _L0_tok_all

    def _L0_attn_setup():
        import jax, jax.numpy as jnp
        import numpy as np
        import math
        N_HEAD = 16
        K_SPARSE = 64
        key = jax.random.key(seed)
        ks = jax.random.split(key, 12)
        B, T, C = (1, 512, 256)
        s = 0.02
        return {'x': jax.random.normal(ks[0], (B, T, C), jnp.float32), 'Wq': jax.random.normal(ks[1], (C, C), jnp.float32) * s, 'bq': jax.random.normal(ks[2], (C,), jnp.float32) * s, 'Wk': jax.random.normal(ks[3], (C, C), jnp.float32) * s, 'bk': jax.random.normal(ks[4], (C,), jnp.float32) * s, 'Wv': jax.random.normal(ks[5], (C, C), jnp.float32) * s, 'bv': jax.random.normal(ks[6], (C,), jnp.float32) * s, 'Wo': jax.random.normal(ks[7], (C, C), jnp.float32) * s, 'bo': jax.random.normal(ks[8], (C,), jnp.float32) * s, 'Wks': jax.random.normal(ks[9], (C,), jnp.float32) * s, 'bks': jax.random.normal(ks[10], (), jnp.float32) * s}
    _L0_attn_all = _L0_attn_setup()
    _L0_attn_in = {k: v for k, v in _L0_attn_all.items() if k in ('Wq', 'bq', 'Wk', 'bk', 'Wv', 'bv', 'Wo', 'bo', 'Wks', 'bks')}
    del _L0_attn_all

    def _L0_ffn_setup():
        import jax, jax.numpy as jnp
        import numpy as np
        D_MODEL = 256
        D_FF = 1024
        N_EXP = 8
        TOP_K = 2

        def _gelu(x):
            return jax.nn.gelu(x, approximate=False)
        key = jax.random.key(seed)
        ks = jax.random.split(key, 12)
        s = 0.02
        return {'x': jax.random.normal(ks[0], (4, 512, D_MODEL), dtype=jnp.float32), 'shared_w1': jax.random.normal(ks[1], (D_MODEL, D_FF), dtype=jnp.float32) * s, 'shared_b1': jnp.zeros((D_FF,), jnp.float32), 'shared_w2': jax.random.normal(ks[2], (D_FF, D_MODEL), dtype=jnp.float32) * s, 'shared_b2': jnp.zeros((D_MODEL,), jnp.float32), 'router_w': jax.random.normal(ks[3], (D_MODEL, N_EXP), dtype=jnp.float32) * s, 'router_b': jnp.zeros((N_EXP,), jnp.float32), 'exp_w1': jax.random.normal(ks[4], (N_EXP, D_MODEL, D_FF), dtype=jnp.float32) * s, 'exp_b1': jnp.zeros((N_EXP, D_FF), jnp.float32), 'exp_w2': jax.random.normal(ks[5], (N_EXP, D_FF, D_MODEL), dtype=jnp.float32) * s, 'exp_b2': jnp.zeros((N_EXP, D_MODEL), jnp.float32)}
    _L0_ffn_all = _L0_ffn_setup()
    _L0_ffn_in = {k: v for k, v in _L0_ffn_all.items() if k in ('shared_w1', 'shared_b1', 'shared_w2', 'shared_b2', 'router_w', 'router_b', 'exp_w1', 'exp_b1', 'exp_w2', 'exp_b2')}
    del _L0_ffn_all
    return {'x': x, 'txt': txt, 'L0_tok_ln1_w': _L0_tok_in['ln1_w'], 'L0_tok_W': _L0_tok_in['W'], 'L0_tok_ln2_w': _L0_tok_in['ln2_w'], 'L0_attn_Wq': _L0_attn_in['Wq'], 'L0_attn_bq': _L0_attn_in['bq'], 'L0_attn_Wk': _L0_attn_in['Wk'], 'L0_attn_bk': _L0_attn_in['bk'], 'L0_attn_Wv': _L0_attn_in['Wv'], 'L0_attn_bv': _L0_attn_in['bv'], 'L0_attn_Wo': _L0_attn_in['Wo'], 'L0_attn_bo': _L0_attn_in['bo'], 'L0_attn_Wks': _L0_attn_in['Wks'], 'L0_attn_bks': _L0_attn_in['bks'], 'L0_ffn_shared_w1': _L0_ffn_in['shared_w1'], 'L0_ffn_shared_b1': _L0_ffn_in['shared_b1'], 'L0_ffn_shared_w2': _L0_ffn_in['shared_w2'], 'L0_ffn_shared_b2': _L0_ffn_in['shared_b2'], 'L0_ffn_router_w': _L0_ffn_in['router_w'], 'L0_ffn_router_b': _L0_ffn_in['router_b'], 'L0_ffn_exp_w1': _L0_ffn_in['exp_w1'], 'L0_ffn_exp_b1': _L0_ffn_in['exp_b1'], 'L0_ffn_exp_w2': _L0_ffn_in['exp_w2'], 'L0_ffn_exp_b2': _L0_ffn_in['exp_b2']}

def reference(x, txt, L0_tok_ln1_w, L0_tok_W, L0_tok_ln2_w, L0_attn_Wq, L0_attn_bq, L0_attn_Wk, L0_attn_bk, L0_attn_Wv, L0_attn_bv, L0_attn_Wo, L0_attn_bo, L0_attn_Wks, L0_attn_bks, L0_ffn_shared_w1, L0_ffn_shared_b1, L0_ffn_shared_w2, L0_ffn_shared_b2, L0_ffn_router_w, L0_ffn_router_b, L0_ffn_exp_w1, L0_ffn_exp_b1, L0_ffn_exp_w2, L0_ffn_exp_b2):
    import jax
    import jax.numpy as jnp

    def _L0_tok_ref(img, ln1_w, W, ln2_w):
        import jax, jax.numpy as jnp
        import numpy as np
        PATCH = 16
        EPS = 1e-05

        def _patchify(img, p):
            B, C, H, W = img.shape
            h, w = (H // p, W // p)
            x = img.reshape(B, C, h, p, w, p)
            x = x.transpose(0, 2, 4, 1, 3, 5)
            return x.reshape(B, h, w, C * p * p)

        def _layernorm(x, gamma):
            mu = x.mean(axis=-1, keepdims=True)
            var = ((x - mu) ** 2).mean(axis=-1, keepdims=True)
            return (x - mu) * jax.lax.rsqrt(var + EPS) * gamma

        def _posemb_sincos_2d(h, w, dim, temperature=10000.0, dtype=jnp.float32):
            y, x = jnp.meshgrid(jnp.arange(h, dtype=dtype), jnp.arange(w, dtype=dtype), indexing='ij')
            omega = jnp.arange(dim // 4, dtype=dtype) / (dim // 4 - 1)
            omega = 1.0 / temperature ** omega
            y = y.reshape(-1)[:, None] * omega[None, :]
            x = x.reshape(-1)[:, None] * omega[None, :]
            return jnp.concatenate([jnp.sin(x), jnp.cos(x), jnp.sin(y), jnp.cos(y)], axis=1)
        patches = _patchify(img, PATCH)
        B, h, w, d = patches.shape
        x = patches.reshape(B, h * w, d)
        x = _layernorm(x, ln1_w)
        x = jnp.einsum('bnd,ed->bne', x, W)
        x = _layernorm(x, ln2_w)
        pe = _posemb_sincos_2d(h, w, x.shape[-1], dtype=x.dtype)
        return x + pe[None, :, :]

    def _L0_attn_ref(x, Wq, bq, Wk, bk, Wv, bv, Wo, bo, Wks, bks):
        import jax, jax.numpy as jnp
        import numpy as np
        import math
        N_HEAD = 16
        K_SPARSE = 64
        B, T, C = x.shape
        nh = N_HEAD
        hs = C // nh
        k_val = min(K_SPARSE, T)
        q = (x @ Wq.T + bq).reshape(B, T, nh, hs).transpose(0, 2, 1, 3)
        k = (x @ Wk.T + bk).reshape(B, T, nh, hs).transpose(0, 2, 1, 3)
        v = (x @ Wv.T + bv).reshape(B, T, nh, hs).transpose(0, 2, 1, 3)
        key_scores = x @ Wks + bks
        pos = jnp.arange(T)
        causal = pos[None, :] <= pos[:, None]
        masked = jnp.where(causal[None], key_scores[:, None, :], -jnp.inf)
        _, top_k_idx = jax.lax.top_k(masked, k_val)
        top_k_idx = jnp.minimum(top_k_idx, pos[None, :, None])
        bi = jnp.arange(B)[:, None, None, None]
        hi = jnp.arange(nh)[None, :, None, None]
        gi = top_k_idx[:, None, :, :]
        sparse_k = k[bi, hi, gi]
        sparse_v = v[bi, hi, gi]
        scale = 1.0 / math.sqrt(hs)
        logits = jnp.einsum('bhtd,bhtkd->bhtk', q, sparse_k) * scale
        probs = jax.nn.softmax(logits, axis=-1)
        out = jnp.einsum('bhtk,bhtkd->bhtd', probs, sparse_v)
        out = out.transpose(0, 2, 1, 3).reshape(B, T, C)
        return out @ Wo.T + bo

    def _L0_ffn_ref(x, shared_w1, shared_b1, shared_w2, shared_b2, router_w, router_b, exp_w1, exp_b1, exp_w2, exp_b2):
        import jax, jax.numpy as jnp
        import numpy as np
        D_MODEL = 256
        D_FF = 1024
        N_EXP = 8
        TOP_K = 2

        def _gelu(x):
            return jax.nn.gelu(x, approximate=False)
        leading = x.shape[:-1]
        d = x.shape[-1]
        xf = x.reshape(-1, d)
        T = xf.shape[0]
        h_shared = _gelu(xf @ shared_w1 + shared_b1) @ shared_w2 + shared_b2
        logits = xf @ router_w + router_b
        routing = jax.nn.softmax(logits, axis=-1)
        sel_w, sel_idx = jax.lax.top_k(routing, TOP_K)
        sel_w = sel_w / (jnp.sum(sel_w, axis=-1, keepdims=True) + 1e-09)
        combine = jnp.zeros((T, N_EXP), routing.dtype)
        combine = combine.at[jnp.arange(T)[:, None], sel_idx].add(sel_w)
        residual = jnp.zeros_like(xf)
        for e in range(N_EXP):
            h = _gelu(xf @ exp_w1[e] + exp_b1[e])
            y = h @ exp_w2[e] + exp_b2[e]
            residual = residual + combine[:, e:e + 1] * y
        out = h_shared + residual
        return out.reshape(*leading, d)
    h = _L0_tok_ref(x, L0_tok_ln1_w, L0_tok_W, L0_tok_ln2_w)
    h = jnp.concatenate([h, txt], axis=1)
    h = h + _L0_attn_ref(_layernorm(h, axis=-1), L0_attn_Wq, L0_attn_bq, L0_attn_Wk, L0_attn_bk, L0_attn_Wv, L0_attn_bv, L0_attn_Wo, L0_attn_bo, L0_attn_Wks, L0_attn_bks)
    h = h + _L0_ffn_ref(_layernorm(h, axis=-1), L0_ffn_shared_w1, L0_ffn_shared_b1, L0_ffn_shared_w2, L0_ffn_shared_b2, L0_ffn_router_w, L0_ffn_router_b, L0_ffn_exp_w1, L0_ffn_exp_b1, L0_ffn_exp_w2, L0_ffn_exp_b2)
    return h

_drawn_inputs = setup_inputs


def setup_inputs(seed=0):
    import zlib

    import numpy as np

    out = dict(_drawn_inputs(seed))
    spreads = {'L0_ffn_shared_b1': (0.0, 0.309),
     'L0_ffn_shared_b2': (0.0, 0.1),
     'L0_ffn_router_b': (0.0, 0.1),
     'L0_ffn_exp_b1': (0.0, 0.395),
     'L0_ffn_exp_b2': (0.0, 0.1)}
    factors = {'L0_attn_Wq': 8.0,
     'L0_attn_bq': 35.917,
     'L0_attn_Wk': 8.0,
     'L0_attn_bk': 64.0,
     'L0_attn_bv': 8.0,
     'L0_attn_bo': 3.175,
     'L0_attn_Wks': 64.0}
    for name, (base, spread) in spreads.items():
        noise = np.random.default_rng([zlib.crc32(name.encode()), seed]).standard_normal(out[name].shape)
        drawn = base * np.exp(spread * noise) if base else spread * noise
        out[name] = jnp.asarray(drawn.astype(out[name].dtype))
    for name, factor in factors.items():
        out[name] = (out[name] * factor).astype(out[name].dtype)
    return out
```

```python
from contextlib import ExitStack

import numpy as np
import concourse.bass as bass
from concourse import mybir

F32 = mybir.dt.float32
BF16 = mybir.dt.bfloat16
I32 = mybir.dt.int32
U32 = mybir.dt.uint32
ALU = mybir.AluOpType
ACT = mybir.ActivationFunctionType
AX = mybir.AxisListType

P = 128
IMAGES, CHANNELS, SIDE, PATCH = 32, 3, 64, 16
GRID = SIDE // PATCH
IMG_TOK = GRID * GRID
TXT_TOK = 32
SEQ = IMG_TOK + TXT_TOK
D = 256
KD = D // P
PD = CHANNELS * PATCH * PATCH
KP = PD // P
HEADS, HS = 16, 16
FF = 1024
KF = FF // P
EXPERTS, TOP = 8, 2
EPS = 1e-5
TOKENS = IMAGES * SEQ
TILES = TOKENS // P
ROUNDS = 4
R_IMG = IMAGES // ROUNDS
R_TOK = R_IMG * SEQ
R_TILES = R_TOK // P
UNITS = 8
SLOT_TILES = TOP * TOKENS // P + EXPERTS - 1
ALL_TILES = TILES + SLOT_TILES
ORDERS = 1 + EXPERTS
RING = 3
W1_AT, W2_AT = 0, KD * FF
B1_AT = W2_AT + KF * D
B2_AT = B1_AT + FF
SLOT = B2_AT + D
KPAD = 64


def stand_alone(carrier):
    dst, src, copy = carrier
    copy(dst, src)


PRIMED = 1


def prime(engine, *sems):
    for s in sems:
        engine.sem_inc(s, PRIMED)


class Chain:

    def __init__(self, engine, sem):
        self.engine, self.sem, self.n, self.base = engine, sem, 0, 0

    def ends(self, ins):
        ins.then_inc(self.sem, 1)
        self.n += 1
        return self

    def settled(self):
        self.engine.wait_ge(self.sem, self.base + self.n)

    def settled_alone(self, spare):
        self.settled()
        stand_alone(spare)

    def loop(self, i, first, per_round):
        self.base, self.n = first + i * per_round, 0

    def leave(self, first, per_round, rounds):
        assert self.n == per_round, (self.n, per_round)
        self.base, self.n = 0, first + per_round * rounds


def program(nc, a, out, stop=None, dbg=None):
    ctx = ExitStack()
    with ctx:
        def sb(name, shape, dt=F32):
            return ctx.enter_context(nc.sbuf_tensor(name, shape, dt))

        def sem(name):
            return ctx.enter_context(nc.semaphore(name))

        def dram(name, shape):
            return nc.dram_tensor(name, shape, F32, kind="Internal").ap()

        rows = dram("rows", [ALL_TILES * P, D])
        ys = dram("ys", [ALL_TILES * P, D])

        ps = ctx.enter_context(nc.psum_tensor("ps", [P, 8, 512], F32))
        ident = sb("ident", [P, P])
        attn_bias = sb("attn_bias", [2 * SEQ, SEQ])
        parity = sb("parity", [P, 4])
        pos = sb("pos", [P, D])
        tri = sb("tri", [P, P], BF16)
        ones = sb("ones", [P, P], BF16)
        small = sb("small", [P, 64])
        vcols = sb("vcols", [P, 12])
        ln2_w = sb("ln2_w", [P, D])
        bo = sb("bo", [P, D])
        rb = sb("rb", [P, EXPERTS])
        rw = sb("rw", [P, KD, EXPERTS])
        w_t = sb("w_t", [P, 4, KD, D])
        px = sb("px", [P, ROUNDS, PD])
        pn = sb("pn", [P, ROUNDS, PD])
        pn_t = sb("pn_t", [P, KP, ROUNDS, P])
        tw_t = sb("tw_t", [P, KP, D])
        h = sb("h", [P, TILES, D])
        xf = sb("xf", [P, TILES, D])
        ring = sb("ring", [P, RING, SLOT])
        xn = sb("xn", [P, R_TILES, D])
        hb = sb("hb", [P, R_TILES, D])
        xn_t = sb("xn_t", [P, KD, R_TOK + KPAD - SEQ])
        qx = sb("qx", [P, KD, R_IMG, 2, SEQ])
        k_t = sb("k_t", [P, KD, R_TOK])
        v = sb("v", [P, R_IMG, P])
        lg = sb("lg", [2 * SEQ, 2, 8, SEQ])
        pr = sb("pr", [2 * SEQ, 2, 8, KPAD])
        mx = sb("mx", [2 * SEQ, 2, 8])
        sm = sb("sm", [2 * SEQ, 2, 8])
        rs = sb("rs", [2 * SEQ, 2, 8])
        p_t = sb("p_t", [KPAD + SEQ, 2, 4 * 2 * SEQ])
        o_odd = sb("o_odd", [P, KD, 4 * SEQ])
        o_t = sb("o_t", [P, KD, R_TILES, P])
        xf_s = sb("xf_s", [P, R_TILES, D])
        xf_t = sb("xf_t", [P, R_TILES, KD, P])
        bn = sb("bn", [P, 8, 6])
        mv = sb("mv", [P, 4, 2])
        ve = sb("ve", [P, 4])
        rstd = sb("rstd", [P, 4])
        half = sb("half", [P, 4])
        pad = sb("pad", [1, 16])
        g_max = sb("g_max", [P, R_TILES, 8])
        g_lg = sb("g_lg", [P, R_TILES, EXPERTS])
        g_exp = sb("g_exp", [P, R_TILES, EXPERTS])
        g_red = sb("g_red", [P, R_TILES])
        g_rec = sb("g_rec", [P, R_TILES])
        g_prob = sb("g_prob", [P, R_TILES, EXPERTS])
        g_idx = sb("g_idx", [P, R_TILES, 8], U32)
        g_idf = sb("g_idf", [P, R_TILES, TOP])
        pick = sb("pick", [P, TOP, TILES, EXPERTS])
        gate = sb("gate", [P, TILES, TOP])
        cnt = sb("cnt", [P, TILES, EXPERTS], BF16)
        n_e = sb("n_e", [P, EXPERTS])
        n_cmp = sb("n_cmp", [P, EXPERTS, TILES])
        n_til = sb("n_til", [P, EXPERTS])
        one8 = sb("one8", [P, EXPERTS])
        end = sb("end", [P, EXPERTS])
        base = sb("base", [P, EXPERTS])
        where = sb("where", [P, TILES, EXPERTS])
        wsel = sb("wsel", [P, TILES, EXPERTS])
        slot_f = sb("slot_f", [P, TOP, TILES])
        slot_i = sb("slot_i", [P, TOP, TILES], I32)
        t_cmp = sb("t_cmp", [1, SLOT_TILES, EXPERTS - 1])
        order_f = sb("order_f", [1, ALL_TILES])
        need = sb("need", [1, ALL_TILES], I32)
        at = sb("at", [1, ALL_TILES], I32)
        t_sub = sb("t_sub", [1, ALL_TILES, 2])
        free_f = sb("free_f", [1, EXPERTS])
        free_i = sb("free_i", [1, EXPERTS], I32)
        zero = sb("zero", [P, D])
        xs = sb("xs", [P, D])
        x_t = sb("x_t", [P, KD, P])
        spare = px[:].rearrange("p i d -> p (i d)")
        hp, hg = spare[:, 0:FF], spare[:, FF:2 * FF]
        h_t = spare[:, 2 * FF:3 * FF].rearrange("p (k c) -> p k c", k=KF)
        y = sb("y", [P, D])
        ysh = pn[:, 0:2, 0:D]
        yr = pn[:, 2:4, 0:TOP * D].rearrange("p b (c d) -> p b c d", c=TOP)

        S = {n: sem(n) for n in (
            "c_loaded", "px_loaded", "w_loaded", "txt_loaded", "r0_loaded", "r1_loaded", "r2_loaded",
            "zeroed", "zero_set", "ones_set", "vec", "pool",
            "w_put", "pn_ready", "pn_tr", "pn_put", "tok_mm", "tok_taken", "tok_done",
            "ve_ready", "rstd_ready", "xn_ready", "xn_tr", "xn_put", "proj", "proj_put", "v_mm", "v_put",
            "scores", "logits", "shifted", "expd", "recip", "probs", "pr_tr", "pt_put", "av", "o_put",
            "wo_mm", "hb_ready", "h_ready", "xf_ready", "xf_kept", "xf_tr", "xf_put", "rt_mm", "rt_lg", "rt_exp",
            "xf_stored", "rank_mm", "cnt_ready", "slots_ready", "scattered", "weights_ready",
            "xs_loaded", "x_tr", "x_put", "l1", "hp_ready", "gelu", "h_tr", "ht_put", "l2", "y_ready",
            "y_stored", "ysh0_loaded", "ysh1_loaded", "yr0_loaded", "yr1_loaded", "combined", "out_stored")}
        ysh_loaded = [S["ysh0_loaded"], S["ysh1_loaded"]]
        yr_loaded = [S["yr0_loaded"], S["yr1_loaded"]]
        ring_loaded = [S["r0_loaded"], S["r1_loaded"], S["r2_loaded"]]

        block = ctx.enter_context(nc.Block())

        C_LOADS = 10

        def weights_of(o):
            if o == 0:
                return a["shared_w1"], a["shared_w2"], a["shared_b1"], a["shared_b2"]
            return tuple(a[n][o - 1] for n in ("exp_w1", "exp_w2", "exp_b1", "exp_b2"))

        def tile_rows(dst, j):
            i, n = divmod(j, R_TILES)
            if n == 0:
                return dst[R_IMG * i:R_IMG * (i + 1), 0:IMG_TOK, :]
            b = R_IMG * i + 4 * (n - 1)
            return dst[b:b + 4, IMG_TOK:SEQ, :]

        @block.sync
        def _(sp):
            for i in range(ROUNDS):
                sp.dma_start(px[:, i], a["patches"][P * i:P * (i + 1), :]).then_inc(S["px_loaded"], 16)
            sp.dma_start(xs[:, 0:P], a["c_tri"]).then_inc(S["w_loaded"], 16)
            sp.dma_start(tw_t[:], a["tok_w"].rearrange("(k p) d -> p k d", p=P)).then_inc(S["w_loaded"], 16)
            for n, name in enumerate(("wq", "wk", "wv", "wo")):
                sp.dma_start(w_t[:, n], a[name].rearrange("(k p) d -> p k d", p=P)).then_inc(S["w_loaded"], 16)
            for i in range(ROUNDS):
                sp.dma_start(h[:, R_TILES * i + 1:R_TILES * i + 3, :],
                             a["txt"].rearrange("b s d -> (b s) d")[2 * P * i:2 * P * (i + 1)]
                             .rearrange("(n p) d -> p n d", p=P)).then_inc(S["txt_loaded"], 16)
            if stop == "tok":
                return
            rows_v = rows.rearrange("(t p) d -> p t d", p=P)
            for i in range(ROUNDS):
                sp.wait_ge(S["xf_kept"], PRIMED + R_TILES * (i + 1))
                sp.dma_start(rows_v[:, R_TILES * i:R_TILES * (i + 1), :], xf[:, R_TILES * i:R_TILES * (i + 1), :])\
                    .then_inc(S["xf_stored"], 16)
            if stop == "attn":
                sp.wait_ge(S["xf_stored"], 16 * ROUNDS)
                return
            sp.wait_ge(S["xf_stored"], 16 * ROUNDS)

            ys_v = ys.rearrange("(t p) d -> t p d", p=P)
            rows_t = rows.rearrange("(t p) d -> t p d", p=P)

            def load(t, first=False):
                if not first:
                    sp.wait_ge(S["x_tr"], t)
                sp.dma_start(xs[:], rows_t[bass.ds(t, 1)].rearrange("o p d -> (o p) d")).then_inc(S["xs_loaded"], 16)

            def store(t):
                sp.wait_ge(S["y_ready"], t + 1)
                sp.dma_start(ys_v[bass.ds(t, 1)].rearrange("o p d -> (o p) d"), y[:]).then_inc(S["y_stored"], 16)

            load(0, first=True)
            for t in range(1, 4):
                load(t)
            with sp.Fori(4, TILES) as t:
                load(t)
                store(t - 4)
            sp.wait_ge(S["scattered"], 16 * TOP * TILES)
            with sp.Fori(TILES, ALL_TILES) as t:
                load(t)
                store(t - 4)
            for t in range(ALL_TILES - 4, ALL_TILES):
                store(t)
            for j in range(TILES):
                if j >= 2:
                    sp.wait_ge(S["combined"], j - 1)
                else:
                    sp.wait_ge(S["y_stored"], 16 * ALL_TILES)
                sp.dma_start(ysh[:, j % 2, :], ys_v[j]).then_inc(ysh_loaded[j % 2], 16)
                if j >= 1:
                    sp.wait_ge(S["combined"], j)
                    sp.dma_start(tile_rows(out, j - 1), h[:, j - 1, :]).then_inc(S["out_stored"], 16)
            sp.wait_ge(S["combined"], TILES)
            sp.dma_start(tile_rows(out, TILES - 1), h[:, TILES - 1, :]).then_inc(S["out_stored"], 16)
            sp.wait_ge(S["out_stored"], 16 * TILES)

        @block.gpsimd
        def _(pool):
            g = nc.gpsimd
            prime(pool, S["probs"], S["xf_kept"])
            g.memset(zero[:], 0.0).then_inc(S["zero_set"], 1)
            g.memset(half[:], -0.5).then_inc(S["pool"], 1)
            g.memset(one8[:], 1.0).then_inc(S["ones_set"], 1)
            g.memset(pr[:], 0.0).then_inc(S["pool"], 1)
            g.memset(xn_t[:, :, R_TOK:], 0.0).then_inc(S["ones_set"], 1)
            g.memset(order_f[:], 0.0).then_inc(S["ones_set"], 1)

            def load_weights(o):
                w1, w2, b1, b2 = weights_of(o)
                s = o % RING
                done = ring_loaded[s]
                g.dma_start(ring[:, s, W1_AT:W2_AT].rearrange("p (k f) -> p k f", k=KD),
                            w1.rearrange("(k p) f -> p k f", p=P)).then_inc(done, 16)
                g.dma_start(ring[:, s, W2_AT:B1_AT].rearrange("p (k d) -> p k d", k=KF),
                            w2.rearrange("(k p) d -> p k d", p=P)).then_inc(done, 16)
                g.dma_start(ring[:, s, B1_AT:B2_AT], b1.partition_broadcast(P)).then_inc(done, 16)
                g.dma_start(ring[:, s, B2_AT:SLOT], b2.partition_broadcast(P)).then_inc(done, 16)

            def tell_weights(o):
                pool.wait_ge(ring_loaded[o % RING], 64 * (o // RING + 1))
                pool.sem_inc(S["weights_ready"], 1)

            for o in range(RING):
                load_weights(o)

            def inverse_root(n, k):
                pool.wait_ge(S["ve_ready"], k)
                g.tensor_tensor(rstd[:, 0:n], ve[:, 0:n], half[:, 0:n], ALU.pow).then_inc(S["rstd_ready"], 1)

            pool.wait_ge(S["pool"], 2)
            inverse_root(4, 1)
            inverse_root(4, 2)
            if stop == "tok":
                return
            with pool.Fori(0, ROUNDS) as i:
                inverse_root(R_TILES, 2 * i + 3)
                pool.wait_ge(S["xn_ready"], R_TILES * (i + 1))
                for n in range(R_TILES):
                    g.tensor_tensor(hb[:, n, :], h[:, bass.ds(R_TILES * i + n, 1), :].rearrange("p o d -> p (o d)"),
                                    bo[:], ALU.add).then_inc(S["hb_ready"], 1)
                for u in range(UNITS):
                    pool.wait_ge(S["recip"], UNITS * i + u + 1)
                    if u >= 2:
                        pool.wait_ge(S["pr_tr"], PRIMED + UNITS * i + u - 1)
                    else:
                        pool.wait_ge(S["pr_tr"], PRIMED + UNITS * i)
                    b = u % 2
                    g.tensor_tensor(pr[:, b, :, 0:SEQ], lg[:, b],
                                    rs[:, b].unsqueeze(2).broadcast_to([2 * SEQ, 8, SEQ]), ALU.mult)\
                        .then_inc(S["probs"], 1)
                inverse_root(R_TILES, 2 * i + 4)
                for n in range(R_TILES):
                    pool.wait_ge(S["xf_ready"], PRIMED + R_TILES * i + n + 1)
                    g.tensor_copy(xf[:, bass.ds(R_TILES * i + n, 1), :].rearrange("p o d -> p (o d)"), xf_s[:, n, :])\
                        .then_inc(S["xf_kept"], 1)
            if stop == "attn":
                for o in range(RING):
                    tell_weights(o)
                return
            pool.wait_ge(S["zeroed"], 16)
            pool.wait_ge(S["slots_ready"], 1)
            pool.wait_ge(S["xf_kept"], PRIMED + TILES)
            for j in range(TILES):
                for c in range(TOP):
                    g.indirect_dma_start(rows, bass.IndirectOffsetOnAxis(slot_i[:, c, j:j + 1], 0),
                                         xf[:, j, :], None).then_inc(S["scattered"], 16)
            for o in range(RING):
                tell_weights(o)
            for o in range(RING, ORDERS):
                if o == RING:
                    pool.wait_ge(S["y_ready"], TILES)
                else:
                    done = pool.value_load(free_i[0:1, o - RING - 1:o - RING], min_val=TILES, max_val=ALL_TILES)
                    pool.wait_ge(S["y_ready"], done)
                    g.tensor_tensor(pad[0:1, o:o + 1], half[0:1, 0:1], half[0:1, 1:2], ALU.add)
                load_weights(o)
                tell_weights(o)
            pool.wait_ge(S["y_stored"], 16 * ALL_TILES)
            for j in range(TILES):
                if j >= 2:
                    pool.wait_ge(S["combined"], j - 1)
                for c in range(TOP):
                    g.indirect_dma_start(yr[:, j % 2, c, :], None, ys,
                                         bass.IndirectOffsetOnAxis(slot_i[:, c, j:j + 1], 0))\
                        .then_inc(yr_loaded[j % 2], 16)

        @block.scalar
        def _(act):
            s = nc.scalar
            prime(act, S["pt_put"], S["xf_put"])
            for dst, src in ((ident, a["c_ident"]), (vcols, a["vcols"]), (small, a["c_small"]),
                             (parity, a["c_parity"]), (pos, a["c_pos"]), (attn_bias, a["c_bias"]),
                             (ln2_w, a["ln2_w"].partition_broadcast(P)), (bo, a["bo"].partition_broadcast(P)),
                             (rb, a["rb"].partition_broadcast(P)), (rw, a["rw"].rearrange("(k p) e -> p k e", p=P))):
                act.dma_start(dst[:], src).then_inc(S["c_loaded"], 16)
            act.wait_ge(S["zero_set"], 1)
            act.dma_start(rows.rearrange("(t p) d -> p t d", p=P)[:, TILES:, :],
                          zero[:].unsqueeze(1).broadcast_to([P, SLOT_TILES, D])).then_inc(S["zeroed"], 16)

            if stop == "tok":
                return
            act.wait_ge(S["ones_set"], 3)
            with act.Fori(0, ROUNDS) as i:
                def xn_tile(n):
                    act.wait_ge(S["xn_tr"], R_TILES * i + n + 1)
                    src = ps[:, 4 + n, 0:KD * P].rearrange("p (k c) -> p k c", k=KD)
                    for k in range(KD):
                        dst = xn_t[:, k, 0:R_TOK].rearrange("p (b t) -> p b t", t=SEQ)
                        if n == 0:
                            o = s.copy(dst[:, :, 0:IMG_TOK], src[:, k].rearrange("p (b t) -> p b t", t=IMG_TOK))
                        else:
                            o = s.copy(dst[:, 4 * (n - 1):4 * n, IMG_TOK:],
                                       src[:, k].rearrange("p (b t) -> p b t", t=TXT_TOK))
                        o.then_inc(S["xn_put"], 1)
                for n in range(R_TILES):
                    xn_tile(n)
                for k in range(KD):
                    act.wait_ge(S["proj"], 4 * i + 2 + k + 1)
                    s.activation(k_t[:, k, :], ps[:, 2 + k, 0:R_TOK], ACT.Identity, bias=vcols[:, 8 + k:9 + k])\
                        .then_inc(S["proj_put"], 1)
                for n in range(2):
                    act.wait_ge(S["v_mm"], 2 * i + n + 1)
                    s.copy(v[:, 4 * n:4 * n + 4, :].rearrange("p b c -> p (b c)"), ps[:, 6 + n, :])\
                        .then_inc(S["v_put"], 1)

                def exps(u):
                    act.wait_ge(S["shifted"], UNITS * i + u + 1)
                    s.activation(lg[:, u % 2], lg[:, u % 2], ACT.Exp).then_inc(S["expd"], 1)

                def put(u):
                    act.wait_ge(S["pr_tr"], PRIMED + UNITS * i + u + 1)
                    if u >= 2:
                        act.wait_ge(S["av"], PRIMED + UNITS * i + u - 1)
                    else:
                        act.wait_ge(S["av"], PRIMED + UNITS * i)
                    s.copy(p_t[:, u % 2, :], ps[0:KPAD + SEQ, 6 + u % 2, 0:8 * SEQ]).then_inc(S["pt_put"], 1)

                exps(0)
                for u in range(1, UNITS):
                    exps(u)
                    put(u - 1)
                put(UNITS - 1)
                for n in range(R_TILES):
                    act.wait_ge(S["xf_tr"], R_TILES * i + n + 1)
                    s.copy(xf_t[:, n].rearrange("p k c -> p (k c)"), ps[:, 4 + n, 0:KD * P])\
                        .then_inc(S["xf_put"], 1)
                act.wait_ge(S["rt_lg"], PRIMED + i + 1)
                s.activation(g_exp[:], g_lg[:], ACT.Exp).then_inc(S["rt_exp"], 1)
            if stop == "attn":
                return

            def x_evac(t):
                act.wait_ge(S["x_tr"], t + 1)
                s.copy(x_t[:].rearrange("p k c -> p (k c)"), ps[:, 5, 0:KD * P]).then_inc(S["x_put"], 1)

            def h_evac(t):
                act.wait_ge(S["h_tr"], 2 * t + 1)
                s.copy(h_t[:, 0:4].rearrange("p k c -> p (k c)"), ps[:, 2, :]).then_inc(S["ht_put"], 1)

            def gelu(t):
                for n in range(2):
                    act.wait_ge(S["hp_ready"], 2 * t + n + 1)
                    if n == 0:
                        act.wait_ge(S["h_tr"], 2 * t)
                    s.activation(hg[:, 512 * n:512 * (n + 1)], hp[:, 512 * n:512 * (n + 1)], ACT.Gelu)\
                        .then_inc(S["gelu"], 1)

            def gelu0():
                for n in range(2):
                    act.wait_ge(S["hp_ready"], n + 1)
                    s.activation(hg[:, 512 * n:512 * (n + 1)], hp[:, 512 * n:512 * (n + 1)], ACT.Gelu)\
                        .then_inc(S["gelu"], 1)

            x_evac(0)
            x_evac(1)
            gelu0()
            with act.Fori(1, ALL_TILES - 1) as t:
                x_evac(t + 1)
                h_evac(t - 1)
                gelu(t)
            t = ALL_TILES - 1
            h_evac(t - 1)
            gelu(t)
            h_evac(t)

        @block.vector
        def _(dve):
            e = nc.vector
            ch = Chain(dve, S["vec"])
            prime(dve, S["o_put"], S["rt_lg"], S["xf_ready"])
            spare = (pad[0:1, 0:1], half[0:1, 0:1], e.tensor_copy)

            dve.wait_ge(S["px_loaded"], 16 * ROUNDS)
            for i in range(ROUNDS):
                for c in range(2):
                    ch.ends(e.bn_stats(bn[:, 2 * i + c, :], px[:, i, PD // 2 * c:PD // 2 * (c + 1)]))
            ch.settled()
            for i in range(ROUNDS):
                ch.ends(e.bn_aggr(mv[:, i, :], bn[:, 2 * i:2 * i + 2, :]))
            ch.settled()
            e.tensor_scalar(ve[:], mv[:, :, 1], EPS, None, ALU.add).then_inc(S["ve_ready"], 1)
            dve.wait_ge(S["w_loaded"], 16 * 6)
            ch.ends(e.tensor_copy(tri[:], xs[:, 0:P]))
            dve.wait_ge(S["c_loaded"], 16 * C_LOADS)
            for k in range(KP):
                e.tensor_scalar(tw_t[:, k, :], tw_t[:, k, :], vcols[:, k:k + 1], None, ALU.mult)\
                    .then_inc(S["w_put"], 1)
            dve.wait_ge(S["rstd_ready"], 1)
            for i in range(ROUNDS):
                e.tensor_scalar(pn[:, i, :], px[:, i, :], mv[:, i, 0:1], rstd[:, i:i + 1], ALU.subtract, ALU.mult)\
                    .then_inc(S["pn_ready"], 1)
            for k in range(KP):
                dve.wait_ge(S["pn_tr"], k + 1)
                e.tensor_copy(pn_t[:, k].rearrange("p t c -> p (t c)"), ps[:, 7 if k % 2 == 0 else 0, :])\
                    .then_inc(S["pn_put"], 1)
            for i in range(ROUNDS):
                dve.wait_ge(S["tok_mm"], i + 1)
                ch.ends(e.bn_stats(bn[:, i, :], ps[:, 1 + i, 0:D]))
            ch.settled()
            for i in range(ROUNDS):
                ch.ends(e.bn_aggr(mv[:, i, :], bn[:, i, :]))
            ch.settled()
            e.tensor_scalar(ve[:], mv[:, :, 1], EPS, None, ALU.add).then_inc(S["ve_ready"], 1)
            dve.wait_ge(S["rstd_ready"], 2)
            for i in range(ROUNDS):
                ch.ends(e.tensor_scalar(h[:, R_TILES * i, :], ps[:, 1 + i, 0:D], mv[:, i, 0:1], rstd[:, i:i + 1],
                                        ALU.subtract, ALU.mult))
            ch.settled()
            for i in range(ROUNDS):
                ch.ends(e.tensor_tensor(h[:, R_TILES * i, :], h[:, R_TILES * i, :], ln2_w[:], ALU.mult))
            ch.settled()
            for i in range(ROUNDS):
                ch.ends(e.tensor_tensor(h[:, R_TILES * i, :], h[:, R_TILES * i, :], pos[:], ALU.add))
            ch.settled()
            e.memset(ones[:], 1.0).then_inc(S["tok_done"], 1)
            if stop == "tok":
                return
            dve.wait_ge(S["txt_loaded"], 16 * ROUNDS)

            first = ch.n

            def tile_of(buf, t):
                return buf[:, bass.ds(t, 1), :].rearrange("p o d -> p (o d)")

            def norm(i, k, dst, signal):
                ch.settled_alone(spare)
                for n in range(R_TILES):
                    ch.ends(e.bn_stats(bn[:, n, :], tile_of(h, R_TILES * i + n)))
                ch.settled_alone(spare)
                for n in range(R_TILES):
                    ch.ends(e.bn_aggr(mv[:, n, :], bn[:, n, :]))
                ch.settled()
                e.tensor_scalar(ve[:, 0:R_TILES], mv[:, 0:R_TILES, 1], EPS, None, ALU.add).then_inc(S["ve_ready"], 1)
                dve.wait_ge(S["rstd_ready"], k)
                for n in range(R_TILES):
                    e.tensor_scalar(dst(n), tile_of(h, R_TILES * i + n), mv[:, n, 0:1], rstd[:, n:n + 1],
                                    ALU.subtract, ALU.mult).then_inc(S[signal], 1)

            per = 2 * 2 * R_TILES + 2 * UNITS + KD * 2 + R_TILES + 16
            with dve.Fori(0, ROUNDS) as i:
                ch.loop(i, first, per)
                norm(i, 2 * i + 3, lambda n: xn[:, n, :], "xn_ready")
                for k in range(KD):
                    dve.wait_ge(S["proj"], 4 * i + k + 1)
                    for par in range(2):
                        e.tensor_scalar(qx[:, k, :, par, :],
                                        ps[:, k, 0:R_TOK].rearrange("p (b q) -> p b q", q=SEQ), vcols[:, 6 + k:7 + k],
                                        parity[:, 2 + par:3 + par], ALU.add, ALU.mult).then_inc(S["proj_put"], 1)

                def shift(u):
                    b = u % 2
                    if u < 2:
                        dve.wait_ge(S["probs"], PRIMED + UNITS * i)
                    else:
                        dve.wait_ge(S["probs"], PRIMED + UNITS * i + u - 1)
                    dve.wait_ge(S["scores"], UNITS * i + u + 1)
                    e.tensor_tensor(lg[:, b], ps[0:2 * SEQ, u % 4, 0:8 * SEQ].rearrange("p (n k) -> p n k", k=SEQ),
                                    attn_bias[:].unsqueeze(1).broadcast_to([2 * SEQ, 8, SEQ]), ALU.add)\
                        .then_inc(S["logits"], 1)
                    dve.wait_ge(S["logits"], UNITS * i + u + 1)
                    ch.ends(e.reduce_max(mx[:, b], lg[:, b], AX.X))
                    ch.settled()
                    e.tensor_tensor(lg[:, b], lg[:, b], mx[:, b].unsqueeze(2).broadcast_to([2 * SEQ, 8, SEQ]),
                                    ALU.subtract).then_inc(S["shifted"], 1)

                def denominators(u):
                    b = u % 2
                    dve.wait_ge(S["expd"], UNITS * i + u + 1)
                    ch.ends(e.reduce_sum(sm[:, b], lg[:, b], AX.X))
                    ch.settled()
                    e.reciprocal(rs[:, b], sm[:, b]).then_inc(S["recip"], 1)

                def select(g):
                    dve.wait_ge(S["av"], PRIMED + UNITS * i + 4 * g + 4)
                    for k in range(KD):
                        o2 = ps[:, 4 + k, 0:8 * SEQ].rearrange("p (b a q) -> p b a q", b=4, a=2)
                        odd = o_odd[:, k].rearrange("p (b q) -> p b q", b=4)
                        dve.wait_ge(S["o_put"], PRIMED + 8 * i + (4 * g + 2 * k - 2 if g else 0))
                        ch.ends(e.tensor_scalar(odd, o2[:, :, 1, :],
                                                parity[:, 1:2], vcols[:, 10 + k:11 + k], ALU.mult, ALU.add))
                        ch.settled()
                        for dst, at_q, n_q in (
                                (o_t[:, k, 0, 4 * IMG_TOK * g:4 * IMG_TOK * (g + 1)], 0, IMG_TOK),
                                (o_t[:, k, 1 + g, :], IMG_TOK, TXT_TOK)):
                            e.scalar_tensor_tensor(
                                dst.rearrange("p (b q) -> p b q", b=4), o2[:, :, 0, at_q:at_q + n_q], parity[:, 0:1],
                                odd[:, :, at_q:at_q + n_q], ALU.mult, ALU.add).then_inc(S["o_put"], 1)

                shift(0)
                for u in range(1, UNITS):
                    shift(u)
                    denominators(u - 1)
                    if u == 6:
                        select(0)
                denominators(UNITS - 1)
                select(1)
                dve.wait_ge(S["hb_ready"], R_TILES * (i + 1))
                for n in range(R_TILES):
                    dve.wait_ge(S["wo_mm"], R_TILES * i + n + 1)
                    ch.ends(e.tensor_tensor(tile_of(h, R_TILES * i + n), ps[:, n, 0:D], hb[:, n, :], ALU.add))
                dve.wait_ge(S["xf_kept"], PRIMED + R_TILES * i)
                norm(i, 2 * i + 4, lambda n: xf_s[:, n, :], "xf_ready")
                def step(ins):
                    ch.ends(ins)
                    ch.settled()

                R8 = [P, R_TILES, EXPERTS]
                dve.wait_ge(S["rt_mm"], i + 1)
                step(e.tensor_tensor(g_lg[:], ps[:, 3, 0:R_TILES * EXPERTS].rearrange("p (n e) -> p n e", e=EXPERTS),
                                     rb[:].unsqueeze(1).broadcast_to(R8), ALU.add))
                step(e.reduce_max(g_red[:], g_lg[:], AX.X))
                e.tensor_tensor(g_lg[:], g_lg[:], g_red[:].unsqueeze(2).broadcast_to(R8), ALU.subtract)\
                    .then_inc(S["rt_lg"], 1)
                dve.wait_ge(S["rt_exp"], i + 1)
                step(e.reduce_sum(g_red[:], g_exp[:], AX.X))
                step(e.reciprocal(g_rec[:], g_red[:]))
                step(e.tensor_tensor(g_prob[:], g_exp[:], g_rec[:].unsqueeze(2).broadcast_to(R8), ALU.mult))
                stand_alone(spare)
                for n in range(R_TILES):
                    ch.ends(e.max(g_max[:, n], g_prob[:, n]))
                ch.settled_alone(spare)
                for n in range(R_TILES):
                    ch.ends(e.max_index(g_idx[:, n], g_max[:, n], g_prob[:, n]))
                step(e.tensor_tensor(g_red[:], g_max[:, :, 0], g_max[:, :, 1], ALU.add))
                step(e.tensor_scalar(g_red[:], g_red[:], 1e-9, None, ALU.add))
                ch.ends(e.tensor_copy(g_idf[:], g_idx[:, :, 0:TOP]))
                step(e.reciprocal(g_rec[:], g_red[:]))
                ch.ends(e.tensor_tensor(gate[:, bass.ds(R_TILES * i, R_TILES), :], g_max[:, :, 0:TOP],
                                        g_rec[:].unsqueeze(2).broadcast_to([P, R_TILES, TOP]), ALU.mult))
                for c in range(TOP):
                    e.tensor_tensor(pick[:, c, bass.ds(R_TILES * i, R_TILES), :],
                                    small[:, 43:43 + EXPERTS].unsqueeze(1).broadcast_to(R8),
                                    g_idf[:, :, c:c + 1].broadcast_to(R8), ALU.is_equal).then_inc(S["cnt_ready"], 1)
                ch.settled()
                dve.wait_ge(S["cnt_ready"], TOP * (i + 1))
            ch.leave(first, per, ROUNDS)
            if stop == "attn":
                return

            dve.wait_ge(S["cnt_ready"], TOP * ROUNDS)
            e.tensor_tensor(cnt[:], pick[:, 0], pick[:, 1], ALU.add).then_inc(S["cnt_ready"], 1)
            dve.wait_ge(S["rank_mm"], 1)
            ch.ends(e.tensor_copy(n_e[:], ps[:, 7, 0:EXPERTS]))
            ch.settled()
            ch.ends(e.tensor_tensor(n_cmp[:], n_e[:].unsqueeze(2).broadcast_to([P, EXPERTS, TILES]),
                                    small[:, 0:TILES].unsqueeze(1).broadcast_to([P, EXPERTS, TILES]), ALU.is_gt))
            ch.settled()
            ch.ends(e.reduce_sum(n_til[:], n_cmp[:], AX.X))
            ch.settled()
            ch.ends(e.tensor_tensor_scan(end[:], one8[:], n_til[:], 0.0, ALU.mult, ALU.add))
            ch.settled()
            ch.ends(e.tensor_tensor(base[:], end[:], n_til[:], ALU.subtract))
            ch.settled()
            ch.ends(e.tensor_scalar(base[:], base[:], float(P), float(TOKENS), ALU.mult, ALU.add))
            ch.settled()
            ch.ends(e.tensor_tensor(where[:], ps[:, 6, 0:TILES * EXPERTS].rearrange("p (t e) -> p t e", e=EXPERTS),
                                    base[:].unsqueeze(1).broadcast_to([P, TILES, EXPERTS]), ALU.add))
            ch.settled()
            for c in range(TOP):
                ch.ends(e.tensor_tensor(wsel[:], where[:], pick[:, c], ALU.mult))
                ch.settled()
                ch.ends(e.reduce_sum(slot_f[:, c], wsel[:], AX.X))
                ch.settled()
            e.tensor_copy(slot_i[:], slot_f[:]).then_inc(S["slots_ready"], 1)
            ch.ends(e.tensor_tensor(
                t_cmp[:], small[0:1, 12:12 + SLOT_TILES].unsqueeze(2).broadcast_to([1, SLOT_TILES, EXPERTS - 1]),
                end[0:1, 0:EXPERTS - 1].unsqueeze(1).broadcast_to([1, SLOT_TILES, EXPERTS - 1]), ALU.is_ge))
            ch.settled()
            dve.wait_ge(S["ones_set"], 3)
            ch.ends(e.reduce_sum(order_f[:, TILES:], t_cmp[:], AX.X))
            ch.settled()
            ch.ends(e.tensor_scalar(order_f[:, TILES:], order_f[:, TILES:], 1.0, None, ALU.add))
            ch.settled()
            for n in range(2):
                ch.ends(e.tensor_scalar(t_sub[:, :, n], order_f[:], float(RING * (n + 1)), -float(RING),
                                        ALU.is_ge, ALU.mult))
            ch.ends(e.tensor_scalar(need[:], order_f[:], 1.0, None, ALU.add))
            ch.settled()
            ch.ends(e.tensor_tensor(order_f[:], order_f[:], t_sub[:, :, 0], ALU.add))
            ch.settled()
            ch.ends(e.tensor_tensor(order_f[:], order_f[:], t_sub[:, :, 1], ALU.add))
            ch.settled()
            ch.ends(e.tensor_copy(at[:], order_f[:]))
            ch.ends(e.tensor_scalar(free_f[:], end[0:1, :], float(TILES), None, ALU.add))
            ch.settled()
            e.tensor_copy(free_i[:], free_f[:]).then_inc(S["slots_ready"], 1)
            dve.wait_ge(S["slots_ready"], 2)

            def slot_of(t):
                return dve.value_load(at[0:1, bass.ds(t, 1)], min_val=0, max_val=RING - 1)

            def bias1(t, started=True):
                s_ = slot_of(t)
                for n in range(2):
                    dve.wait_ge(S["l1"], 2 * t + n + 1)
                    if started:
                        dve.wait_ge(S["gelu"], 2 * t - 1 + n)
                    e.tensor_tensor(hp[:, 512 * n:512 * (n + 1)], ps[:, n, :],
                                    ring[:, bass.ds(s_, 1), B1_AT + 512 * n:B1_AT + 512 * (n + 1)]
                                    .rearrange("p o f -> p (o f)"), ALU.add).then_inc(S["hp_ready"], 1)

            def h_evac(t):
                dve.wait_ge(S["h_tr"], 2 * t + 2)
                e.tensor_copy(h_t[:, 4:8].rearrange("p k c -> p (k c)"), ps[:, 3, :]).then_inc(S["ht_put"], 1)

            def bias2(t, stored=True):
                s_ = slot_of(t)
                dve.wait_ge(S["l2"], t + 1)
                if stored:
                    dve.wait_ge(S["y_stored"], 16 * t)
                e.tensor_tensor(y[:], ps[:, 4, 0:D], ring[:, bass.ds(s_, 1), B2_AT:SLOT]
                                .rearrange("p o f -> p (o f)"), ALU.add).then_inc(S["y_ready"], 1)

            bias1(0, started=False)
            bias1(1)
            h_evac(0)
            bias1(2)
            bias2(0, stored=False)
            h_evac(1)
            with dve.Fori(3, ALL_TILES) as t:
                bias1(t)
                bias2(t - 2)
                h_evac(t - 1)
            bias2(ALL_TILES - 2)
            h_evac(ALL_TILES - 1)
            bias2(ALL_TILES - 1)

            for j in range(TILES):
                dve.wait_ge(ysh_loaded[j % 2], 16 * (j // 2 + 1))
                ch.ends(e.tensor_tensor(h[:, j, :], h[:, j, :], ysh[:, j % 2, :], ALU.add))
                ch.settled()
                dve.wait_ge(yr_loaded[j % 2], 16 * TOP * (j // 2 + 1))
                ch.ends(e.scalar_tensor_tensor(h[:, j, :], yr[:, j % 2, 0, :], gate[:, j, 0:1], h[:, j, :],
                                               ALU.mult, ALU.add))
                ch.settled()
                e.scalar_tensor_tensor(h[:, j, :], yr[:, j % 2, 1, :], gate[:, j, 1:2], h[:, j, :],
                                       ALU.mult, ALU.add).then_inc(S["combined"], 1)

        @block.tensor
        def _(pe):
            t_ = nc.tensor
            prime(pe, S["av"], S["pr_tr"])
            pe.wait_ge(S["c_loaded"], 16 * C_LOADS)
            pe.wait_ge(S["pn_ready"], ROUNDS)
            for k in range(KP):
                if k >= 2:
                    pe.wait_ge(S["pn_put"], k - 1)
                for i in range(ROUNDS):
                    last = t_.transpose(ps[:, 7 if k % 2 == 0 else 0, P * i:P * (i + 1)],
                                        pn[:, i, P * k:P * (k + 1)], ident[:])
                last.then_inc(S["pn_tr"], 1)
            pe.wait_ge(S["w_put"], KP)
            pe.wait_ge(S["pn_put"], KP)
            for i in range(ROUNDS):
                for k in range(KP):
                    last = t_.matmul(ps[:, 1 + i, 0:D], pn_t[:, k, i, :], tw_t[:, k, :], start=k == 0, stop=k == KP - 1)
                last.then_inc(S["tok_mm"], 1)
            if stop == "tok":
                return
            pe.wait_ge(S["tok_done"], 1)
            with pe.Fori(0, ROUNDS) as i:
                pe.wait_ge(S["o_put"], PRIMED + 8 * i)
                pe.wait_ge(S["xf_put"], PRIMED + R_TILES * i)
                for n in range(R_TILES):
                    pe.wait_ge(S["xn_ready"], R_TILES * i + n + 1)
                    for k in range(KD):
                        last = t_.transpose(ps[:, 4 + n, P * k:P * (k + 1)], xn[:, n, P * k:P * (k + 1)], ident[:])
                    last.then_inc(S["xn_tr"], 1)
                pe.wait_ge(S["xn_put"], KD * R_TILES * (i + 1))
                pe.wait_ge(S["rt_lg"], PRIMED + i)
                pe.wait_ge(S["xf_ready"], PRIMED + R_TILES * i)
                for n in range(4):
                    w, r = divmod(n, 2)
                    for k in range(KD):
                        last = t_.matmul(ps[:, n, 0:R_TOK], w_t[:, w, k, P * r:P * (r + 1)], xn_t[:, k, 0:R_TOK],
                                         start=k == 0, stop=k == KD - 1)
                    last.then_inc(S["proj"], 1)
                pe.wait_ge(S["pt_put"], PRIMED + UNITS * i)
                for n in range(2):
                    for b in range(4):
                        for r in range(KD):
                            for k in range(KD):
                                at_b = SEQ * (4 * n + b)
                                last = t_.matmul(ps[KPAD * r:KPAD * (r + 1), 6 + n, P * b:P * (b + 1)],
                                                 xn_t[:, k, at_b:at_b + KPAD], w_t[:, 2, k, P * r:P * (r + 1)],
                                                 start=k == 0, stop=k == KD - 1)
                    last.then_inc(S["v_mm"], 1)

                def scores(u):
                    g, r = divmod(u, 4)
                    if u < 4:
                        if u == 0:
                            pe.wait_ge(S["proj_put"], 6 * (i + 1))
                    else:
                        pe.wait_ge(S["logits"], UNITS * i + u - 3)
                    for b in range(4):
                        for k in range(KD):
                            c = SEQ * (4 * g + b)
                            last = t_.matmul(ps[0:2 * SEQ, r, SEQ * (2 * b + k):SEQ * (2 * b + k + 1)],
                                             qx[32 * r:32 * (r + 1), k, 4 * g + b].rearrange("p a q -> p (a q)"),
                                             k_t[32 * r:32 * (r + 1), k, c:c + SEQ], start=True, stop=True)
                    last.then_inc(S["scores"], 1)

                def transpose_probs(u):
                    b2 = u % 2
                    pe.wait_ge(S["probs"], PRIMED + UNITS * i + u + 1)
                    if u == 0:
                        pe.wait_ge(S["v_put"], 2 * (i + 1))
                    else:
                        pe.wait_ge(S["pt_put"], PRIMED + UNITS * i + u)
                    if u == 5:
                        pe.wait_ge(S["o_put"], PRIMED + 8 * i + 4)
                    for b in range(4):
                        last = t_.transpose(ps[0:KPAD + SEQ, 6 + b2, 2 * SEQ * b:2 * SEQ * (b + 1)],
                                            pr[:, b2, 2 * b:2 * b + 2, :].rearrange("p n k -> p (n k)")
                                            [:, 0:KPAD + SEQ], ident[0:2 * SEQ, 0:2 * SEQ])
                    last.then_inc(S["pr_tr"], 1)

                def attend(u):
                    g, r = divmod(u, 4)
                    for b in range(4):
                        for k in range(KD):
                            last = t_.matmul(ps[32 * r:32 * (r + 1), 4 + k, 2 * SEQ * b:2 * SEQ * (b + 1)],
                                             v[KPAD * k:KPAD * k + SEQ, 4 * g + b, 32 * r:32 * (r + 1)],
                                             p_t[KPAD * k:KPAD * k + SEQ, u % 2, 2 * SEQ * b:2 * SEQ * (b + 1)],
                                             start=True, stop=True)
                    last.then_inc(S["av"], 1)

                for u in range(3):
                    scores(u)
                for u in range(UNITS):
                    if u + 3 < UNITS:
                        scores(u + 3)
                    transpose_probs(u)
                    if u:
                        attend(u - 1)
                pe.wait_ge(S["pt_put"], PRIMED + UNITS * (i + 1))
                t_.matmul(ps[:, 7, 0:P], ident[:], ident[:], start=True, stop=True)
                attend(UNITS - 1)
                pe.wait_ge(S["logits"], UNITS * (i + 1))
                pe.wait_ge(S["o_put"], PRIMED + 8 * (i + 1))
                for n in range(R_TILES):
                    for k in range(KD):
                        last = t_.matmul(ps[:, n, 0:D], o_t[:, k, n, :], w_t[:, 3, k, :], start=k == 0, stop=k == KD - 1)
                    last.then_inc(S["wo_mm"], 1)
                for n in range(R_TILES):
                    pe.wait_ge(S["xf_ready"], PRIMED + R_TILES * i + n + 1)
                    for k in range(KD):
                        last = t_.transpose(ps[:, 4 + n, P * k:P * (k + 1)],
                                            xf_s[:, n, P * k:P * (k + 1)], ident[:])
                    last.then_inc(S["xf_tr"], 1)
                for n in range(R_TILES):
                    pe.wait_ge(S["xf_put"], PRIMED + R_TILES * i + n + 1)
                    for k in range(KD):
                        last = t_.matmul(ps[:, 3, 8 * n:8 * n + 8], xf_t[:, n, k, :], rw[:, k, :],
                                         start=k == 0, stop=k == KD - 1)
                last.then_inc(S["rt_mm"], 1)
            if stop == "attn":
                return

            pe.wait_ge(S["cnt_ready"], TOP * ROUNDS + 1)
            pe.wait_ge(S["ones_set"], 3)
            last = t_.matmul(ps[:, 6, 0:TILES * EXPERTS], tri[:], cnt[:].rearrange("p t e -> p (t e)"),
                             start=True, stop=False)
            for j in range(TILES - 1):
                last = t_.matmul(ps[:, 6, EXPERTS * (j + 1):EXPERTS * TILES].rearrange("p (t e) -> p t e", e=EXPERTS),
                                 ones[:], cnt[:, j:j + 1, :].broadcast_to([P, TILES - 1 - j, EXPERTS]),
                                 start=False, stop=j == TILES - 2)
            for j in range(TILES):
                last = t_.matmul(ps[:, 7, 0:EXPERTS], ones[:], cnt[:, j, :], start=j == 0, stop=j == TILES - 1)
            last.then_inc(S["rank_mm"], 1)

            pe.wait_ge(S["slots_ready"], 2)

            def x_transpose(t, first=False):
                pe.wait_ge(S["xs_loaded"], 16 * (t + 1))
                if not first:
                    pe.wait_ge(S["x_put"], t)
                for k in range(KD):
                    last = t_.transpose(ps[:, 5, P * k:P * (k + 1)], xs[:, P * k:P * (k + 1)], ident[:])
                last.then_inc(S["x_tr"], 1)

            def slot_of(t):
                return pe.value_load(at[0:1, bass.ds(t, 1)], min_val=0, max_val=RING - 1)

            def layer1(t):
                n_w = pe.value_load(need[0:1, bass.ds(t, 1)], min_val=1, max_val=ORDERS)
                s_ = slot_of(t)
                pe.wait_ge(S["weights_ready"], n_w)
                pe.wait_ge(S["x_put"], t + 1)
                pe.wait_ge(S["hp_ready"], 2 * t)
                for n in range(2):
                    for k in range(KD):
                        w_at = W1_AT + FF * k + 512 * n
                        last = t_.matmul(ps[:, n, :], x_t[:, k, :],
                                         ring[:, bass.ds(s_, 1), w_at:w_at + 512].rearrange("p o f -> p (o f)"),
                                         start=k == 0, stop=k == KD - 1)
                    last.then_inc(S["l1"], 1)

            def h_transpose(t):
                pe.wait_ge(S["ht_put"], 2 * t)
                for n in range(2):
                    pe.wait_ge(S["gelu"], 2 * t + n + 1)
                    for k in range(4):
                        c = P * (4 * n + k)
                        last = t_.transpose(ps[:, 2 + n, P * k:P * (k + 1)], hg[:, c:c + P], ident[:])
                    last.then_inc(S["h_tr"], 1)

            def layer2(t):
                s_ = slot_of(t)
                pe.wait_ge(S["ht_put"], 2 * t + 2)
                pe.wait_ge(S["y_ready"], t)
                for k in range(KF):
                    w_at = W2_AT + D * k
                    last = t_.matmul(ps[:, 4, 0:D], h_t[:, k, :],
                                     ring[:, bass.ds(s_, 1), w_at:w_at + D].rearrange("p o f -> p (o f)"),
                                     start=k == 0, stop=k == KF - 1)
                last.then_inc(S["l2"], 1)

            x_transpose(0, first=True)
            layer1(0)
            x_transpose(1)
            layer1(1)
            x_transpose(2)
            h_transpose(0)
            with pe.Fori(2, ALL_TILES - 1) as t:
                layer1(t)
                x_transpose(t + 1)
                layer2(t - 2)
                h_transpose(t - 1)
            t = ALL_TILES - 1
            layer1(t)
            layer2(t - 2)
            h_transpose(t - 1)
            layer2(t - 1)
            h_transpose(t)
            layer2(t)


_NAMES = {"txt": "txt", "ln2_w": "L0_tok_ln2_w", "bo": "L0_attn_bo",
          "shared_w1": "L0_ffn_shared_w1", "shared_b1": "L0_ffn_shared_b1", "shared_w2": "L0_ffn_shared_w2",
          "shared_b2": "L0_ffn_shared_b2", "rw": "L0_ffn_router_w", "rb": "L0_ffn_router_b",
          "exp_w1": "L0_ffn_exp_w1", "exp_b1": "L0_ffn_exp_b1", "exp_w2": "L0_ffn_exp_w2", "exp_b2": "L0_ffn_exp_b2"}


def constants():
    f = np.float32
    q, k = np.arange(SEQ)[:, None], np.arange(SEQ)[None, :]
    times = np.log(SEQ - q).astype(f)
    bias = np.where(k < q, f(0), np.where(k == q, times, f(-1e30))).astype(f)
    odd = ((np.arange(P) // HS) % 2).astype(f)
    parity = np.stack([1 - odd, odd, (1 - odd) * f(HS ** -0.5), odd * f(HS ** -0.5)], 1).astype(f)
    small = np.zeros((P, 64), f)
    small[:, 0:TILES] = P * np.arange(TILES)
    small[:, 12:12 + SLOT_TILES] = np.arange(SLOT_TILES)
    small[:, 43:43 + EXPERTS] = np.arange(EXPERTS)
    small[:, 63] = -0.5
    omega = np.arange(D // 4, dtype=f) / f(D // 4 - 1)
    omega = (f(1) / np.power(f(10000.0), omega)).astype(f)
    yy, xx = np.meshgrid(np.arange(GRID, dtype=f), np.arange(GRID, dtype=f), indexing="ij")
    ya, xa = yy.reshape(-1)[:, None] * omega, xx.reshape(-1)[:, None] * omega
    pe = np.concatenate([np.sin(xa), np.cos(xa), np.sin(ya), np.cos(ya)], 1).astype(f)
    return {"c_ident": np.eye(P, dtype=f), "c_bias": np.tile(bias, (2, 1)), "c_parity": parity, "c_small": small,
            "c_pos": np.tile(pe, (P // IMG_TOK, 1)),
            "c_tri": (np.arange(P)[:, None] < np.arange(P)[None, :]).astype(f)}


def laid_out(inputs):
    x = np.asarray(inputs["x"]).reshape(IMAGES, CHANNELS, GRID, PATCH, GRID, PATCH)
    turned = {"tok_w": "L0_tok_W", "wq": "L0_attn_Wq", "wk": "L0_attn_Wk", "wv": "L0_attn_Wv", "wo": "L0_attn_Wo"}
    vectors = ("L0_tok_ln1_w", "L0_attn_bq", "L0_attn_bk", "L0_attn_bv")
    return {"patches": np.ascontiguousarray(x.transpose(0, 2, 4, 1, 3, 5)).reshape(IMAGES * IMG_TOK, PD),
            "vcols": np.ascontiguousarray(
                np.concatenate([np.asarray(inputs[n]).reshape(-1, P) for n in vectors], 0).T),
            **{k: np.ascontiguousarray(np.asarray(inputs[n]).T) for k, n in turned.items()}}


def build(nc, inputs, **kw):
    arrays, aps = {}, {}
    given = {k: np.ascontiguousarray(inputs[v]) for k, v in _NAMES.items()}
    for name, arr in {**given, **laid_out(inputs), **constants()}.items():
        arrays[f"in_{name}"] = arr
        aps[name] = nc.dram_tensor(f"in_{name}", arr.shape, mybir.dt.from_np(arr.dtype), kind="ExternalInput").ap()
    out = nc.dram_tensor("out_0", (IMAGES, SEQ, D), F32, kind="ExternalOutput").ap()
    program(nc, aps, out, **kw)
    return arrays


def kernel(**inputs):
    import concourse.bacc as bacc
    from concourse.bass_utils import run_bass_kernel_spmd

    nc = bacc.Bacc("TRN2", target_bir_lowering=False, num_devices=1)
    arrays = build(nc, inputs)
    r = run_bass_kernel_spmd(nc, [arrays], core_ids=[0])
    return r.results[0]["out_0"]
```

```python
from contextlib import ExitStack

import numpy as np
import concourse.bass as bass
from concourse import mybir

F32 = mybir.dt.float32
BF16 = mybir.dt.bfloat16
F32R = mybir.dt.float32r
I32 = mybir.dt.int32
U32 = mybir.dt.uint32
ALU = mybir.AluOpType
ACT = mybir.ActivationFunctionType
AX = mybir.AxisListType

P = 128
IMAGES, CHANNELS, SIDE, PATCH = 32, 3, 64, 16
GRID = SIDE // PATCH
IMG_TOK = GRID * GRID
TXT_TOK = 32
SEQ = IMG_TOK + TXT_TOK
D = 256
KD = D // P
PD = CHANNELS * PATCH * PATCH
KP = PD // P
HEADS, HS = 16, 16
FF = 1024
KF = FF // P
EXPERTS, TOP = 8, 2
EPS = 1e-5
TOKENS = IMAGES * SEQ
TILES = TOKENS // P
ROUNDS = 4
R_IMG = IMAGES // ROUNDS
R_TOK = R_IMG * SEQ
R_TILES = R_TOK // P
UNITS = 8
SLOT_TILES = TOP * TOKENS // P + EXPERTS - 1
ALL_TILES = TILES + SLOT_TILES
FIRST = TILES // 2
SORTED = FIRST + SLOT_TILES
ORDERS = EXPERTS + 2
RING = 2
W1_AT, W2_AT = 0, KD * FF
SPLIT = W2_AT + KF * D
PIECE = 1024
KPAD = 64


def reach(engine, sem, n):
    if n > 0:
        engine.wait_ge(sem, n)


class Chain:

    def __init__(self, engine, sem):
        self.engine, self.sem, self.n, self.base = engine, sem, 0, 0

    def ends(self, ins):
        ins.then_inc(self.sem, 1)
        self.n += 1
        return self

    def settled(self):
        self.engine.wait_ge(self.sem, self.base + self.n)

    def loop(self, i, first, per_round):
        self.base, self.n = first + i * per_round, 0

    def leave(self, first, per_round, rounds):
        assert self.n == per_round, (self.n, per_round)
        self.base, self.n = 0, first + per_round * rounds


def program(nc, a, out):
    ctx = ExitStack()
    with ctx:
        def sb(name, shape, dt=F32):
            return ctx.enter_context(nc.sbuf_tensor(name, shape, dt))

        def sem(name):
            return ctx.enter_context(nc.semaphore(name))

        def dram(name, shape):
            return nc.dram_tensor(name, shape, F32, kind="Internal").ap()

        own = dram("own", [TOKENS, D])
        rows = dram("rows", [SLOT_TILES * P, D])
        ys = dram("ys", [SLOT_TILES * P, D])

        ps = ctx.enter_context(nc.psum_tensor("ps", [P, 8, 512], F32))
        ident = sb("ident", [P, P])
        attn_bias = sb("attn_bias", [2 * SEQ, SEQ])
        parity = sb("parity", [P, 4])
        pos = sb("pos", [P, D])
        tri = sb("tri", [P, P], BF16)
        ones = sb("ones", [P, P], BF16)
        small = sb("small", [P, 64])
        vcols = sb("vcols", [P, 12])
        ln2_w = sb("ln2_w", [P, D])
        bo = sb("bo", [P, D])
        rb = sb("rb", [P, EXPERTS])
        rw = sb("rw", [P, KD, EXPERTS])
        w_t = sb("w_t", [P, 4, KD, D])
        h = sb("h", [P, TILES, D])
        xf = sb("xf", [P, TILES, D])
        ring = sb("ring", [P, RING, 2 * SPLIT], F32R)
        b1s = sb("b1s", [P, RING, FF])
        b2s = sb("b2s", [P, RING, D])
        xn = sb("xn", [P, R_TILES, D])
        xn_t = sb("xn_t", [P, KD, R_IMG, KPAD])
        lg = sb("lg", [2 * SEQ, 2, 8, SEQ])
        pr = sb("pr", [2 * SEQ, 2, 8, KPAD])
        mx = sb("mx", [2 * SEQ, 2, 8])
        sm = sb("sm", [2 * SEQ, 2, 8])
        rs = sb("rs", [2 * SEQ, 2, 8])
        p_t = sb("p_t", [KPAD + SEQ, 2, 4 * 2 * SEQ])
        o_odd = sb("o_odd", [P, KD, 4 * SEQ])
        o_t = sb("o_t", [P, KD, R_TILES, P])
        xf_s = sb("xf_s", [P, R_TILES, D])
        xf_t = sb("xf_t", [P, R_TILES, KD, P])
        bn = sb("bn", [P, 8, 6])
        mv = sb("mv", [P, 4, 2])
        ve = sb("ve", [P, 4])
        rstd = sb("rstd", [P, 4])
        half = sb("half", [P, 4])
        pad = sb("pad", [1, 16])
        g_max = sb("g_max", [P, R_TILES, 8])
        g_lg = sb("g_lg", [P, R_TILES, EXPERTS])
        g_exp = sb("g_exp", [P, R_TILES, EXPERTS])
        g_red = sb("g_red", [P, R_TILES])
        g_rec = sb("g_rec", [P, R_TILES])
        g_prob = sb("g_prob", [P, R_TILES, EXPERTS])
        g_idx = sb("g_idx", [P, R_TILES, 8], U32)
        g_idf = sb("g_idf", [P, R_TILES, TOP])
        pick = sb("pick", [P, TOP, TILES, EXPERTS])
        gate = sb("gate", [P, TILES, TOP])
        cnt = sb("cnt", [P, TILES, EXPERTS], BF16)
        n_e = sb("n_e", [P, EXPERTS])
        n_cmp = sb("n_cmp", [P, EXPERTS, TILES])
        n_til = sb("n_til", [P, EXPERTS])
        one8 = sb("one8", [P, EXPERTS])
        end = sb("end", [P, EXPERTS])
        base = sb("base", [P, EXPERTS])
        where = sb("where", [P, TILES, EXPERTS])
        wsel = sb("wsel", [P, TILES, EXPERTS])
        slot_f = sb("slot_f", [P, TOP, TILES])
        slot_i = sb("slot_i", [P, TOP, TILES], I32)
        t_cmp = sb("t_cmp", [1, SLOT_TILES, EXPERTS - 1])
        order_f = sb("order_f", [1, ALL_TILES])
        at_f = sb("at_f", [1, ALL_TILES])
        need = sb("need", [1, ALL_TILES], I32)
        at = sb("at", [1, ALL_TILES], I32)
        t_alt = sb("t_alt", [1, SLOT_TILES, EXPERTS - 1])
        free_f = sb("free_f", [1, EXPERTS])
        free_i = sb("free_i", [1, 2, EXPERTS], I32)
        with ExitStack() as early:
            def sb_early(name, shape):
                return early.enter_context(nc.sbuf_tensor(name, shape, F32))

            px = sb_early("px", [P, ROUNDS, PD])
            pn = sb_early("pn", [P, ROUNDS, PD])
            pn_t = sb_early("pn_t", [P, KP, ROUNDS, P])
            tw_t = sb_early("tw_t", [P, KP, D])
        raw = sb("raw", [P, SPLIT])
        with ExitStack() as middle:
            def sb_middle(name, shape):
                return middle.enter_context(nc.sbuf_tensor(name, shape, F32))

            qx = sb_middle("qx", [P, 2, KD, R_IMG, 2, SEQ])
            k_t = sb_middle("k_t", [P, 2, KD, R_TOK])
            v = sb_middle("v", [P, 2, R_IMG // 2, D])
        hp = sb("hp", [P, FF])
        hg = sb("hg", [P, FF])
        h_hi = sb("h_hi", [P, KF, P], F32R)
        h_lo = sb("h_lo", [P, KF, P], F32R)
        x_hi = sb("x_hi", [P, KD, P], F32R)
        x_lo = sb("x_lo", [P, KD, P], F32R)
        xs = sb("xs", [P, D])
        y = sb("y", [P, D])
        yr = sb("yr", [P, 2, TOP, D])
        sm_tri = xf_t[:, 0, 0, :]

        S = {n: sem(n) for n in (
            "c_loaded", "px_loaded", "w_loaded", "txt_loaded", "raw1_loaded", "raw2_loaded",
            "b1_0", "b1_1", "b2_0", "b2_1", "w_hi", "w_lo", "pad_set",
            "zeroed", "zero_set", "ones_set", "vec", "pool", "ve_tail", "rstd_tail",
            "w_put", "pn_ready", "pn_tr", "pn_put", "tok_mm", "tok_taken", "tok_done",
            "ve_ready", "rstd_ready", "xn_ready", "xn_tr", "xn_put", "proj", "q_put", "k_put", "v_mm", "v_put",
            "scores", "logits", "shifted", "expd", "recip", "probs", "pr_tr", "pt_put", "av", "o_put",
            "wo_mm", "hb_ready", "h_new", "xf_ready", "xf_kept", "xf_tr", "xf_put", "rt_mm", "rt_read", "rt_lg", "rt_exp",
            "xf_stored", "rank_mm", "cnt_ready", "slots_ready", "scattered", "w1_ready", "w2_ready",
            "xs_loaded", "x_tr", "x_high", "x_put", "l1", "hp_ready", "gelu", "h_tr", "ht_hi", "ht_put", "l2", "y_ready",
            "y_stored", "yr0_loaded", "yr1_loaded", "combined", "out_stored")}
        yr_loaded = [S["yr0_loaded"], S["yr1_loaded"]]
        b1_loaded, b2_loaded = [S["b1_0"], S["b1_1"]], [S["b2_0"], S["b2_1"]]

        SIDE_BANK = {"T": (6, 7, 6), "W": (7, 6, 7), "Q": (6, 7), "X": (6, 7, 6), "R": (7,), "K": (6, 7), "V": (6, 7)}

        def xn_puts(i, n):
            return KD * ((R_TILES + 1) * i + (n + 1 if n else 0))

        COMBINED = [j for b in range(FIRST) for j in (b, FIRST + b)]

        block = ctx.enter_context(nc.Block())

        C_LOADS = 10

        def weights_of(o):
            if o in (0, ORDERS - 1):
                return a["shared_w1"], a["shared_w2"], a["shared_b1"], a["shared_b2"]
            return tuple(a[n][o - 1] for n in ("exp_w1", "exp_w2", "exp_b1", "exp_b2"))

        def tile_rows(dst, j):
            i, n = divmod(j, R_TILES)
            if n == 0:
                return dst[R_IMG * i:R_IMG * (i + 1), 0:IMG_TOK, :]
            b = R_IMG * i + 4 * (n - 1)
            return dst[b:b + 4, IMG_TOK:SEQ, :]

        @block.sync
        def _(sp):
            for i in range(ROUNDS):
                sp.dma_start(px[:, i], a["patches"][P * i:P * (i + 1), :]).then_inc(S["px_loaded"], 16)
            sp.dma_start(sm_tri, a["c_tri"]).then_inc(S["w_loaded"], 16)
            sp.dma_start(tw_t[:], a["tok_w"].rearrange("(k p) d -> p k d", p=P)).then_inc(S["w_loaded"], 16)
            for n, name in enumerate(("wq", "wk", "wv", "wo")):
                sp.dma_start(w_t[:, n], a[name].rearrange("(k p) d -> p k d", p=P)).then_inc(S["w_loaded"], 16)
            for i in range(ROUNDS):
                sp.dma_start(h[:, R_TILES * i + 1:R_TILES * i + 3, :],
                             a["txt"].rearrange("b s d -> (b s) d")[2 * P * i:2 * P * (i + 1)]
                             .rearrange("(n p) d -> p n d", p=P)).then_inc(S["txt_loaded"], 16)
            own_v = own.rearrange("(t p) d -> p t d", p=P)
            for i in range(ROUNDS):
                sp.wait_ge(S["xf_kept"], R_TILES * (i + 1))
                sp.dma_start(own_v[:, R_TILES * i:R_TILES * (i + 1), :], xf[:, R_TILES * i:R_TILES * (i + 1), :])\
                    .then_inc(S["xf_stored"], 16)
            sp.wait_ge(S["xf_stored"], 16 * ROUNDS)

            ys_v = ys.rearrange("(t p) d -> t p d", p=P)
            rows_t = rows.rearrange("(t p) d -> t p d", p=P)
            own_t = own.rearrange("(t p) d -> t p d", p=P)

            def load(t, table, row, first=False):
                if not first:
                    sp.wait_ge(S["x_tr"], t)
                sp.dma_start(xs[:], table[bass.ds(row, 1)].rearrange("o p d -> (o p) d")).then_inc(S["xs_loaded"], 16)

            def store(n):
                sp.wait_ge(S["y_ready"], FIRST + n + 1)
                sp.dma_start(ys_v[bass.ds(n, 1)].rearrange("o p d -> (o p) d"), y[:]).then_inc(S["y_stored"], 16)

            load(0, own_t, 0, first=True)
            with sp.Fori(1, FIRST) as t:
                load(t, own_t, t)
            sp.wait_ge(S["scattered"], 16 * TOP * TILES)
            for n in range(4):
                load(FIRST + n, rows_t, n)
            with sp.Fori(4, SLOT_TILES) as n:
                load(FIRST + n, rows_t, n)
                store(n - 4)
            for n in range(4):
                load(SORTED + n, own_t, FIRST + n)
                store(SLOT_TILES - 4 + n)
            for n in range(4, FIRST):
                load(SORTED + n, own_t, FIRST + n)
            for n, j in enumerate(COMBINED):
                sp.wait_ge(S["combined"], n + 1)
                sp.dma_start(tile_rows(out, j), h[:, j, :]).then_inc(S["out_stored"], 16)
            sp.wait_ge(S["out_stored"], 16 * TILES)

        @block.gpsimd
        def _(pool):
            g = nc.gpsimd
            g.memset(xf_s[:, 0, :], 0.0).then_inc(S["zero_set"], 1)
            g.memset(half[:], -0.5).then_inc(S["pool"], 1)
            g.memset(one8[:], 1.0).then_inc(S["ones_set"], 1)
            g.memset(pr[:], 0.0).then_inc(S["pool"], 1)
            g.memset(xn_t[:, :, :, SEQ:], 0.0).then_inc(S["ones_set"], 1)
            g.memset(order_f[:], 0.0).then_inc(S["ones_set"], 1)
            g.memset(at_f[:], 0.0).then_inc(S["ones_set"], 1)

            W_DST = ((raw[:, W1_AT:W2_AT].rearrange("p (k f) -> p k f", k=KD), S["raw1_loaded"]),
                     (raw[:, W2_AT:SPLIT].rearrange("p (k d) -> p k d", k=KF), S["raw2_loaded"]))

            def load_raw(o, layer):
                dst, loaded = W_DST[layer]
                g.dma_start(dst, weights_of(o)[layer].rearrange("(k p) c -> p k c", p=P)).then_inc(loaded, 16)

            def load_bias(o, layer):
                dst, loaded = ((b1s, b1_loaded), (b2s, b2_loaded))[layer]
                g.dma_start(dst[:, o % RING, :], weights_of(o)[2 + layer].partition_broadcast(P))\
                    .then_inc(loaded[o % RING], 16)

            def split_piece(o, c):
                return (lambda low: ring[:, o % RING, PIECE * c + low:PIECE * (c + 1) + low],
                        raw[:, PIECE * c:PIECE * (c + 1)])

            def high_part(dst, piece):
                g.tensor_scalar(dst(0), piece, 1.0, 0.0, ALU.mult, ALU.add).then_inc(S["w_hi"], 1)

            def low_part(dst, piece, n):
                pool.wait_ge(S["w_hi"], n + 1)
                g.tensor_tensor(dst(SPLIT), piece, dst(0).bitcast(F32), ALU.subtract).then_inc(S["w_lo"], 1)

            PIECES = SPLIT // PIECE

            def split_layer(o, layer):
                pool.wait_ge(W_DST[layer][1], 16 * (o + 1))
                for c in range(PIECES // 2 * layer, PIECES // 2 * (layer + 1)):
                    dst, piece = split_piece(o, c)
                    high_part(dst, piece)
                    low_part(dst, piece, PIECES * o + c)
                pool.wait_ge(S["w_lo"], PIECES * o + PIECES // 2 * (layer + 1))

            def tell_weights(o, layer):
                pool.wait_ge((b1_loaded, b2_loaded)[layer][o % RING], 16 * (o // RING + 1))
                pool.sem_inc((S["w1_ready"], S["w2_ready"])[layer], 1)

            for o in range(RING):
                for layer in range(2):
                    load_bias(o, layer)

            def inverse_root(n, k, ready="ve_ready", done="rstd_ready"):
                pool.wait_ge(S[ready], k)
                g.tensor_tensor(rstd[:, 0:n], ve[:, 0:n], half[:, 0:n], ALU.pow).then_inc(S[done], 1)

            pool.wait_ge(S["pool"], 2)
            inverse_root(4, 1)
            inverse_root(4, 2)
            pool.wait_ge(S["tok_done"], 1)
            for layer in range(2):
                load_raw(0, layer)

            def head_root(i):
                inverse_root(R_TILES, 3 + i)

            def head_bias(i):
                pool.wait_ge(S["xn_ready"], R_TILES * (i + 1))
                for n in range(R_TILES):
                    h_n = h[:, R_TILES * i + n, :]
                    g.tensor_tensor(h_n, h_n, bo[:], ALU.add).then_inc(S["hb_ready"], 1)

            def multiply(n):
                if n < 0:
                    return
                pool.wait_ge(S["recip"], n + 1)
                reach(pool, S["pr_tr"], n - 1)
                g.tensor_tensor(pr[:, n % 2, :, 0:SEQ], lg[:, n % 2],
                                rs[:, n % 2].unsqueeze(2).broadcast_to([2 * SEQ, 8, SEQ]), ALU.mult)\
                    .then_inc(S["probs"], 1)

            def tail_root(i):
                inverse_root(R_TILES, i + 1, "ve_tail", "rstd_tail")

            def keep(i, n):
                pool.wait_ge(S["xf_ready"], R_TILES * i + n + 1)
                g.tensor_copy(xf[:, R_TILES * i + n, :], xf_s[:, n, :]).then_inc(S["xf_kept"], 1)

            head_root(0)
            head_bias(0)
            for i in range(ROUNDS):
                before, after = i > 0, i + 1 < ROUNDS
                dst, piece = split_piece(0, i)
                for u in range(UNITS):
                    multiply(UNITS * i + u - 1)
                    if after and u == 0:
                        head_root(i + 1)
                    if after and u == 1:
                        head_bias(i + 1)
                    if u == 3:
                        if i == 0:
                            for layer in range(2):
                                pool.wait_ge(W_DST[layer][1], 16)
                        high_part(dst, piece)
                    if u == 4:
                        low_part(dst, piece, i)
                    if before and u == 5:
                        tail_root(i - 1)
                    if before and u == 7:
                        for n in range(R_TILES):
                            keep(i - 1, n)
            multiply(UNITS * ROUNDS - 1)
            tail_root(ROUNDS - 1)
            for n in range(R_TILES):
                keep(ROUNDS - 1, n)
            pool.wait_ge(S["w_lo"], PIECES)
            for layer in range(2):
                tell_weights(0, layer)
                load_raw(1, layer)
            pool.wait_ge(S["zeroed"], 16)
            pool.wait_ge(S["slots_ready"], 1)
            pool.wait_ge(S["xf_kept"], TILES)
            for j in range(TILES):
                for c in range(TOP):
                    g.indirect_dma_start(rows, bass.IndirectOffsetOnAxis(slot_i[:, c, j:j + 1], 0),
                                         xf[:, j, :], None).then_inc(S["scattered"], 16)
            for o in range(1, ORDERS):
                for layer in range(2):
                    if o >= RING:
                        gone = (S["hp_ready"], S["y_ready"])[layer]
                        if o == RING:
                            pool.wait_ge(gone, (2 - layer) * FIRST)
                        else:
                            e_ = o - RING - 1
                            done = pool.value_load(free_i[0:1, 1 - layer, e_:e_ + 1], min_val=FIRST,
                                                   max_val=2 * ALL_TILES)
                            pool.wait_ge(gone, done)
                            g.tensor_tensor(pad[0:1, o:o + 1], half[0:1, 0:1], half[0:1, 1:2], ALU.add)\
                                .then_inc(S["pad_set"], 1)
                        load_bias(o, layer)
                    split_layer(o, layer)
                    tell_weights(o, layer)
                    if o + 1 < ORDERS:
                        load_raw(o + 1, layer)
            pool.wait_ge(S["y_stored"], 16 * SLOT_TILES)
            for n, j in enumerate(COMBINED):
                if n >= 2:
                    pool.wait_ge(S["combined"], n - 1)
                for c in range(TOP):
                    g.indirect_dma_start(yr[:, n % 2, c, :], None, ys,
                                         bass.IndirectOffsetOnAxis(slot_i[:, c, j:j + 1], 0))\
                        .then_inc(yr_loaded[n % 2], 16)

        @block.scalar
        def _(act):
            s = nc.scalar
            for dst, src in ((ident, a["c_ident"]), (vcols, a["vcols"]), (small, a["c_small"]),
                             (parity, a["c_parity"]), (pos, a["c_pos"]), (attn_bias, a["c_bias"]),
                             (ln2_w, a["ln2_w"].partition_broadcast(P)), (bo, a["bo"].partition_broadcast(P)),
                             (rb, a["rb"].partition_broadcast(P)), (rw, a["rw"].rearrange("(k p) e -> p k e", p=P))):
                act.dma_start(dst[:], src).then_inc(S["c_loaded"], 16)
            act.wait_ge(S["zero_set"], 1)
            act.dma_start(rows.rearrange("(t p) d -> p t d", p=P)[:],
                          xf_s[:, 0, :].unsqueeze(1).broadcast_to([P, SLOT_TILES, D])).then_inc(S["zeroed"], 16)

            act.wait_ge(S["ones_set"], 4)

            def xn_tile(i, n):
                act.wait_ge(S["xn_tr"], R_TILES * i + n + 1)
                src = ps[:, SIDE_BANK["T"][n], 0:KD * P].rearrange("p (k c) -> p k c", k=KD)
                for k in range(KD):
                    for g in ((0, 1), (0,), (1,))[n]:
                        toks, at_t = (IMG_TOK, 0) if n == 0 else (TXT_TOK, IMG_TOK)
                        c = 4 * toks * g if n == 0 else 0
                        s.copy(xn_t[:, k, 4 * g:4 * g + 4, at_t:at_t + toks].rearrange("p (a c) t -> p c a t", a=2),
                               src[:, k, c:c + 4 * toks].rearrange("p (c a t) -> p c a t", c=2, a=2))\
                            .then_inc(S["xn_put"], 1)

            def keys(i, k):
                act.wait_ge(S["proj"], 4 * i + 2 + k + 1)
                s.activation(k_t[:, i % 2, k, :], ps[:, SIDE_BANK["K"][k], 0:R_TOK], ACT.Identity,
                             bias=vcols[:, 8 + k:9 + k]).then_inc(S["k_put"], 1)

            def values(i, n):
                act.wait_ge(S["v_mm"], 2 * i + n + 1)
                s.copy(v[:, i % 2, 2 * n:2 * n + 2, :].rearrange("p b c -> p (b c)"), ps[:, SIDE_BANK["V"][n], :])\
                    .then_inc(S["v_put"], 1)

            def exps(n):
                act.wait_ge(S["shifted"], n + 1)
                s.activation(lg[:, n % 2], lg[:, n % 2], ACT.Exp).then_inc(S["expd"], 1)

            def put(n):
                if n < 0:
                    return
                act.wait_ge(S["pr_tr"], n + 1)
                reach(act, S["av"], n - 1)
                s.copy(p_t[:, n % 2, :], ps[0:KPAD + SEQ, 2 + n % 2, 0:8 * SEQ]).then_inc(S["pt_put"], 1)

            def ffn_input(i, n):
                act.wait_ge(S["xf_tr"], R_TILES * i + n + 1)
                s.copy(xf_t[:, n].rearrange("p k c -> p (k c)"), ps[:, SIDE_BANK["X"][n], 0:KD * P])\
                    .then_inc(S["xf_put"], 1)

            def router_exp(i):
                act.wait_ge(S["rt_lg"], i + 1)
                s.activation(g_exp[:], g_lg[:], ACT.Exp).then_inc(S["rt_exp"], 1)

            for n in range(R_TILES):
                xn_tile(0, n)
            for k in range(KD):
                keys(0, k)
            for i in range(ROUNDS):
                before, after = i > 0, i + 1 < ROUNDS
                for u in range(UNITS):
                    put(UNITS * i + u - 2)
                    exps(UNITS * i + u)
                    if u == 1:
                        if i > 1:
                            router_exp(i - 2)
                        values(i, 0)
                        values(i, 1)
                    if after and u in (2, 3):
                        for n in ((0, 1), (2,))[u - 2]:
                            xn_tile(i + 1, n)
                    if after and u in (6, 7):
                        keys(i + 1, u - 6)
                    if before and u == 7:
                        for n in range(R_TILES):
                            ffn_input(i - 1, n)
            put(UNITS * ROUNDS - 2)
            router_exp(ROUNDS - 2)
            put(UNITS * ROUNDS - 1)
            for n in range(R_TILES):
                ffn_input(ROUNDS - 1, n)
            router_exp(ROUNDS - 1)

            def x_evac(t):
                act.wait_ge(S["x_tr"], t + 1)
                s.copy(x_hi[:].rearrange("p k c -> p (k c)"), ps[:, 5, 0:KD * P]).then_inc(S["x_high"], 1)

            def h_evac(t):
                for n in range(2):
                    act.wait_ge(S["h_tr"], 2 * t + n + 1)
                    s.copy(h_hi[:, 4 * n:4 * n + 4].rearrange("p k c -> p (k c)"), ps[:, 2 + n, :])\
                        .then_inc(S["ht_hi"], 1)

            def gelu(t):
                for n in range(2):
                    act.wait_ge(S["hp_ready"], 2 * t + n + 1)
                    if n == 0:
                        act.wait_ge(S["h_tr"], 2 * t)
                    s.activation(hg[:, 512 * n:512 * (n + 1)], hp[:, 512 * n:512 * (n + 1)], ACT.Gelu)\
                        .then_inc(S["gelu"], 1)

            def gelu0():
                for n in range(2):
                    act.wait_ge(S["hp_ready"], n + 1)
                    s.activation(hg[:, 512 * n:512 * (n + 1)], hp[:, 512 * n:512 * (n + 1)], ACT.Gelu)\
                        .then_inc(S["gelu"], 1)

            x_evac(0)
            x_evac(1)
            gelu0()
            with act.Fori(1, ALL_TILES - 1) as t:
                x_evac(t + 1)
                h_evac(t - 1)
                gelu(t)
            t = ALL_TILES - 1
            h_evac(t - 1)
            gelu(t)
            h_evac(t)

        @block.vector
        def _(dve):
            e = nc.vector
            ch = Chain(dve, S["vec"])

            dve.wait_ge(S["px_loaded"], 16 * ROUNDS)
            for i in range(ROUNDS):
                for c in range(2):
                    ch.ends(e.bn_stats(bn[:, 2 * i + c, :], px[:, i, PD // 2 * c:PD // 2 * (c + 1)]))
            ch.settled()
            for i in range(ROUNDS):
                ch.ends(e.bn_aggr(mv[:, i, :], bn[:, 2 * i:2 * i + 2, :]))
            ch.settled()
            e.tensor_scalar(ve[:], mv[:, :, 1], EPS, None, ALU.add).then_inc(S["ve_ready"], 1)
            dve.wait_ge(S["w_loaded"], 16 * 6)
            ch.ends(e.tensor_copy(tri[:], sm_tri))
            dve.wait_ge(S["c_loaded"], 16 * C_LOADS)
            for k in range(KP):
                e.tensor_scalar(tw_t[:, k, :], tw_t[:, k, :], vcols[:, k:k + 1], None, ALU.mult)\
                    .then_inc(S["w_put"], 1)
            dve.wait_ge(S["rstd_ready"], 1)
            for i in range(ROUNDS):
                e.tensor_scalar(pn[:, i, :], px[:, i, :], mv[:, i, 0:1], rstd[:, i:i + 1], ALU.subtract, ALU.mult)\
                    .then_inc(S["pn_ready"], 1)
            for k in range(KP):
                dve.wait_ge(S["pn_tr"], k + 1)
                e.tensor_copy(pn_t[:, k].rearrange("p t c -> p (t c)"), ps[:, 7 if k % 2 == 0 else 0, :])\
                    .then_inc(S["pn_put"], 1)
            for i in range(ROUNDS):
                dve.wait_ge(S["tok_mm"], i + 1)
                ch.ends(e.bn_stats(bn[:, i, :], ps[:, 1 + i, 0:D]))
            ch.settled()
            for i in range(ROUNDS):
                ch.ends(e.bn_aggr(mv[:, i, :], bn[:, i, :]))
            ch.settled()
            e.tensor_scalar(ve[:], mv[:, :, 1], EPS, None, ALU.add).then_inc(S["ve_ready"], 1)
            dve.wait_ge(S["rstd_ready"], 2)
            for i in range(ROUNDS):
                ch.ends(e.tensor_scalar(h[:, R_TILES * i, :], ps[:, 1 + i, 0:D], mv[:, i, 0:1], rstd[:, i:i + 1],
                                        ALU.subtract, ALU.mult))
            ch.settled()
            for i in range(ROUNDS):
                ch.ends(e.tensor_tensor(h[:, R_TILES * i, :], h[:, R_TILES * i, :], ln2_w[:], ALU.mult))
            ch.settled()
            for i in range(ROUNDS):
                ch.ends(e.tensor_tensor(h[:, R_TILES * i, :], h[:, R_TILES * i, :], pos[:], ALU.add))
            ch.settled()
            e.memset(ones[:], 1.0).then_inc(S["tok_done"], 1)
            dve.wait_ge(S["txt_loaded"], 16 * ROUNDS)

            dve.wait_ge(S["zeroed"], 16)

            def tile_of(buf, t):
                return buf[:, bass.ds(t, 1), :].rearrange("p o d -> p (o d)")

            def spread(i, signal):
                ch.settled()
                for n in range(R_TILES):
                    ch.ends(e.bn_stats(bn[:, n, :], h[:, R_TILES * i + n, :]))
                ch.settled()
                for n in range(R_TILES):
                    ch.ends(e.bn_aggr(mv[:, n, :], bn[:, n, :]))
                ch.settled()
                e.tensor_scalar(ve[:, 0:R_TILES], mv[:, 0:R_TILES, 1], EPS, None, ALU.add).then_inc(S[signal], 1)

            def normalise(i, dst, signal):
                for n in range(R_TILES):
                    e.tensor_scalar(dst[:, n, :], h[:, R_TILES * i + n, :], mv[:, n, 0:1], rstd[:, n:n + 1],
                                    ALU.subtract, ALU.mult).then_inc(S[signal], 1)

            def head_normalise(i):
                dve.wait_ge(S["rstd_ready"], 3 + i)
                normalise(i, xn, "xn_ready")

            def queries(i, k):
                dve.wait_ge(S["proj"], 4 * i + k + 1)
                for par in range(2):
                    e.tensor_scalar(qx[:, i % 2, k, :, par, :],
                                    ps[:, SIDE_BANK["Q"][k], 0:R_TOK].rearrange("p (b q) -> p b q", q=SEQ),
                                    vcols[:, 6 + k:7 + k], parity[:, 2 + par:3 + par], ALU.add, ALU.mult)\
                        .then_inc(S["q_put"], 1)

            def shift(n):
                b = n % 2
                reach(dve, S["probs"], n - 1)
                dve.wait_ge(S["scores"], n + 1)
                e.tensor_tensor(lg[:, b], ps[0:2 * SEQ, b, 0:8 * SEQ].rearrange("p (n k) -> p n k", k=SEQ),
                                attn_bias[:].unsqueeze(1).broadcast_to([2 * SEQ, 8, SEQ]), ALU.add)\
                    .then_inc(S["logits"], 1)
                dve.wait_ge(S["logits"], n + 1)
                ch.ends(e.reduce_max(mx[:, b], lg[:, b], AX.X))
                ch.settled()
                e.tensor_tensor(lg[:, b], lg[:, b], mx[:, b].unsqueeze(2).broadcast_to([2 * SEQ, 8, SEQ]),
                                ALU.subtract).then_inc(S["shifted"], 1)

            def denominators(n):
                if n < 0:
                    return
                b = n % 2
                dve.wait_ge(S["expd"], n + 1)
                ch.ends(e.reduce_sum(sm[:, b], lg[:, b], AX.X))
                ch.settled()
                e.reciprocal(rs[:, b], sm[:, b]).then_inc(S["recip"], 1)

            def select(i, g):
                dve.wait_ge(S["av"], UNITS * i + 4 * g + 4)
                reach(dve, S["wo_mm"], R_TILES * i)
                for k in range(KD):
                    o2 = ps[:, 4:6, :].rearrange("p c (a x) -> p (c a) x", a=2)[:, :, 2 * SEQ * k:2 * SEQ * (k + 1)]\
                        .rearrange("p b (a q) -> p b a q", a=2)
                    odd = o_odd[:, k].rearrange("p (b q) -> p b q", b=4)
                    reach(dve, S["o_put"], 8 * i + 4 * g + 2 * k - 2)
                    ch.ends(e.tensor_scalar(odd, o2[:, :, 1, :],
                                            parity[:, 1:2], vcols[:, 10 + k:11 + k], ALU.mult, ALU.add))
                    ch.settled()
                    for dst, at_q, n_q in (
                            (o_t[:, k, 0, 4 * IMG_TOK * g:4 * IMG_TOK * (g + 1)], 0, IMG_TOK),
                            (o_t[:, k, 1 + g, :], IMG_TOK, TXT_TOK)):
                        e.scalar_tensor_tensor(
                            dst.rearrange("p (b q) -> p b q", b=4), o2[:, :, 0, at_q:at_q + n_q], parity[:, 0:1],
                            odd[:, :, at_q:at_q + n_q], ALU.mult, ALU.add).then_inc(S["o_put"], 1)

            def residual(i, n):
                dve.wait_ge(S["hb_ready"], R_TILES * (i + 1))
                dve.wait_ge(S["wo_mm"], R_TILES * i + n + 1)
                h_n = h[:, R_TILES * i + n, :]
                e.tensor_tensor(h_n, ps[:, SIDE_BANK["W"][n], 0:D], h_n, ALU.add).then_inc(S["h_new"], 1)

            def tail_spread(i):
                dve.wait_ge(S["h_new"], R_TILES * (i + 1))
                spread(i, "ve_tail")

            def tail_normalise(i):
                dve.wait_ge(S["rstd_tail"], i + 1)
                reach(dve, S["xf_kept"], R_TILES * i)
                normalise(i, xf_s, "xf_ready")

            R8 = [P, R_TILES, EXPERTS]

            def step(ins):
                ch.ends(ins)
                ch.settled()

            def router_logits(i):
                dve.wait_ge(S["rt_mm"], i + 1)
                e.tensor_tensor(g_lg[:], ps[:, SIDE_BANK["R"][0], 0:R_TILES * EXPERTS]
                                .rearrange("p (n e) -> p n e", e=EXPERTS),
                                rb[:].unsqueeze(1).broadcast_to(R8), ALU.add).then_inc(S["rt_read"], 1)
                dve.wait_ge(S["rt_read"], i + 1)
                step(e.reduce_max(g_red[:], g_lg[:], AX.X))
                e.tensor_tensor(g_lg[:], g_lg[:], g_red[:].unsqueeze(2).broadcast_to(R8), ALU.subtract)\
                    .then_inc(S["rt_lg"], 1)

            def choose(i):
                dve.wait_ge(S["rt_exp"], i + 1)
                step(e.reduce_sum(g_red[:], g_exp[:], AX.X))
                step(e.reciprocal(g_rec[:], g_red[:]))
                step(e.tensor_tensor(g_prob[:], g_exp[:], g_rec[:].unsqueeze(2).broadcast_to(R8), ALU.mult))
                for n in range(R_TILES):
                    ch.ends(e.max(g_max[:, n], g_prob[:, n]))
                ch.settled()
                for n in range(R_TILES):
                    ch.ends(e.max_index(g_idx[:, n], g_max[:, n], g_prob[:, n]))
                step(e.tensor_tensor(g_red[:], g_max[:, :, 0], g_max[:, :, 1], ALU.add))
                step(e.tensor_scalar(g_red[:], g_red[:], 1e-9, None, ALU.add))
                ch.ends(e.tensor_copy(g_idf[:], g_idx[:, :, 0:TOP]))
                step(e.reciprocal(g_rec[:], g_red[:]))
                ch.ends(e.tensor_tensor(gate[:, R_TILES * i:R_TILES * (i + 1), :], g_max[:, :, 0:TOP],
                                        g_rec[:].unsqueeze(2).broadcast_to([P, R_TILES, TOP]), ALU.mult))
                for c in range(TOP):
                    e.tensor_tensor(pick[:, c, R_TILES * i:R_TILES * (i + 1), :],
                                    small[:, 43:43 + EXPERTS].unsqueeze(1).broadcast_to(R8),
                                    g_idf[:, :, c:c + 1].broadcast_to(R8), ALU.is_equal).then_inc(S["cnt_ready"], 1)
                ch.settled()
                dve.wait_ge(S["cnt_ready"], TOP * (i + 1))

            spread(0, "ve_ready")
            head_normalise(0)
            for k in range(KD):
                queries(0, k)
            for i in range(ROUNDS):
                before, after = i > 0, i + 1 < ROUNDS
                for u in range(UNITS):
                    if u == 6:
                        select(i, 0)
                    shift(UNITS * i + u)
                    denominators(UNITS * i + u - 1)
                    if after and u == 0:
                        spread(i + 1, "ve_ready")
                    if i > 1 and u == 0:
                        router_logits(i - 2)
                    if after and u == 1:
                        head_normalise(i + 1)
                    if i > 1 and u == 1:
                        choose(i - 2)
                    if before and u == 2:
                        select(i - 1, 1)
                    if before and u == 4:
                        residual(i - 1, 0)
                        residual(i - 1, 1)
                    if before and u == 5:
                        residual(i - 1, 2)
                        tail_spread(i - 1)
                    if after and u in (5, 6):
                        queries(i + 1, u - 5)
                    if before and u == 6:
                        tail_normalise(i - 1)
            denominators(UNITS * ROUNDS - 1)
            last = ROUNDS - 1
            router_logits(last - 1)
            choose(last - 1)
            select(last, 1)
            for n in range(R_TILES):
                residual(last, n)
            tail_spread(last)
            tail_normalise(last)
            router_logits(last)
            choose(last)

            dve.wait_ge(S["cnt_ready"], TOP * ROUNDS)
            e.tensor_tensor(cnt[:], pick[:, 0], pick[:, 1], ALU.add).then_inc(S["cnt_ready"], 1)
            dve.wait_ge(S["rank_mm"], 1)
            ch.ends(e.tensor_copy(n_e[:], ps[:, 7, 0:EXPERTS]))
            ch.settled()
            ch.ends(e.tensor_tensor(n_cmp[:], n_e[:].unsqueeze(2).broadcast_to([P, EXPERTS, TILES]),
                                    small[:, 0:TILES].unsqueeze(1).broadcast_to([P, EXPERTS, TILES]), ALU.is_gt))
            ch.settled()
            ch.ends(e.reduce_sum(n_til[:], n_cmp[:], AX.X))
            ch.settled()
            ch.ends(e.tensor_scalar(n_til[:], n_til[:], 1.0, None, ALU.max))
            ch.settled()
            ch.ends(e.tensor_tensor_scan(end[:], one8[:], n_til[:], 0.0, ALU.mult, ALU.add))
            ch.settled()
            ch.ends(e.tensor_tensor(base[:], end[:], n_til[:], ALU.subtract))
            ch.settled()
            ch.ends(e.tensor_scalar(base[:], base[:], float(P), None, ALU.mult))
            ch.settled()
            ch.ends(e.tensor_tensor(where[:], ps[:, 6, 0:TILES * EXPERTS].rearrange("p (t e) -> p t e", e=EXPERTS),
                                    base[:].unsqueeze(1).broadcast_to([P, TILES, EXPERTS]), ALU.add))
            ch.settled()
            for c in range(TOP):
                ch.ends(e.tensor_tensor(wsel[:], where[:], pick[:, c], ALU.mult))
                ch.settled()
                ch.ends(e.reduce_sum(slot_f[:, c], wsel[:], AX.X))
                ch.settled()
            e.tensor_copy(slot_i[:], slot_f[:]).then_inc(S["slots_ready"], 1)
            ch.ends(e.tensor_tensor(
                t_cmp[:], small[0:1, 12:12 + SLOT_TILES].unsqueeze(2).broadcast_to([1, SLOT_TILES, EXPERTS - 1]),
                end[0:1, 0:EXPERTS - 1].unsqueeze(1).broadcast_to([1, SLOT_TILES, EXPERTS - 1]), ALU.is_ge))
            ch.settled()
            dve.wait_ge(S["ones_set"], 4)
            ch.ends(e.reduce_sum(order_f[:, FIRST:SORTED], t_cmp[:], AX.X))
            ch.ends(e.tensor_tensor(t_alt[:], t_cmp[:], small[0:1, 51:50 + EXPERTS].unsqueeze(1)
                                    .broadcast_to([1, SLOT_TILES, EXPERTS - 1]), ALU.mult))
            ch.settled()
            ch.ends(e.reduce_sum(at_f[:, FIRST:SORTED], t_alt[:], AX.X))
            ch.settled()
            ch.ends(e.tensor_scalar(at_f[:, FIRST:SORTED], at_f[:, FIRST:SORTED], -1.0, 1.0, ALU.mult, ALU.add))
            ch.ends(e.tensor_scalar(order_f[:, FIRST:SORTED], order_f[:, FIRST:SORTED], 1.0, None, ALU.add))
            ch.ends(e.tensor_scalar(order_f[:, SORTED:], order_f[:, SORTED:], float(ORDERS - 1), None, ALU.add))
            ch.ends(e.tensor_scalar(at_f[:, SORTED:], at_f[:, SORTED:], float((ORDERS - 1) % RING), None, ALU.add))
            ch.ends(e.tensor_scalar(free_f[:], end[0:1, :], float(FIRST), None, ALU.add))
            ch.settled()
            ch.ends(e.tensor_scalar(need[:], order_f[:], 1.0, None, ALU.add))
            ch.ends(e.tensor_copy(at[:], at_f[:]))
            ch.ends(e.tensor_scalar(free_i[:, 1, :], free_f[:], 2.0, None, ALU.mult))
            ch.settled()
            e.tensor_copy(free_i[:, 0, :], free_f[:]).then_inc(S["slots_ready"], 1)
            dve.wait_ge(S["slots_ready"], 2)

            def slot_of(t):
                return dve.value_load(at[0:1, bass.ds(t, 1)], min_val=0, max_val=RING - 1)

            def x_evac(t):
                dve.wait_ge(S["x_high"], t + 1)
                e.tensor_tensor(x_lo[:].rearrange("p k c -> p (k c)"), ps[:, 5, 0:KD * P],
                                x_hi[:].rearrange("p k c -> p (k c)").bitcast(F32), ALU.subtract)\
                    .then_inc(S["x_put"], 1)

            def bias1(t, started=True):
                s_ = slot_of(t)
                for n in range(2):
                    dve.wait_ge(S["l1"], 2 * t + n + 1)
                    if started:
                        dve.wait_ge(S["gelu"], 2 * t - 1 + n)
                    e.tensor_tensor(hp[:, 512 * n:512 * (n + 1)], ps[:, n, :],
                                    b1s[:, bass.ds(s_, 1), 512 * n:512 * (n + 1)]
                                    .rearrange("p o f -> p (o f)"), ALU.add).then_inc(S["hp_ready"], 1)

            def h_evac(t):
                for n in range(2):
                    dve.wait_ge(S["ht_hi"], 2 * t + n + 1)
                    e.tensor_tensor(h_lo[:, 4 * n:4 * n + 4].rearrange("p k c -> p (k c)"), ps[:, 2 + n, :],
                                    h_hi[:, 4 * n:4 * n + 4].rearrange("p k c -> p (k c)").bitcast(F32),
                                    ALU.subtract).then_inc(S["ht_put"], 1)

            def bias2(t):
                s_ = slot_of(t)
                dve.wait_ge(S["l2"], t + 1)
                e.tensor_tensor(y[:], ps[:, 4, 0:D], b2s[:, bass.ds(s_, 1), :]
                                .rearrange("p o f -> p (o f)"), ALU.add).then_inc(S["y_ready"], 1)

            def shared_out(t, h_j):
                ch.settled()
                bias2(t)
                dve.wait_ge(S["y_ready"], t + 1)
                ch.ends(e.tensor_tensor(h_j, h_j, y[:], ALU.add))

            def sorted_out(t):
                dve.wait_ge(S["y_stored"], 16 * (t - FIRST))
                bias2(t)

            def combine(n):
                j = COMBINED[n]
                dve.wait_ge(yr_loaded[n % 2], 16 * TOP * (n // 2 + 1))
                ch.settled()
                ch.ends(e.scalar_tensor_tensor(h[:, j, :], yr[:, n % 2, 0, :], gate[:, j, 0:1], h[:, j, :],
                                               ALU.mult, ALU.add))
                ch.settled()
                e.scalar_tensor_tensor(h[:, j, :], yr[:, n % 2, 1, :], gate[:, j, 1:2], h[:, j, :],
                                       ALU.mult, ALU.add).then_inc(S["combined"], 1)

            x_evac(0)
            bias1(0, started=False)
            x_evac(1)
            bias1(1)
            x_evac(2)
            h_evac(0)
            first = ch.n
            with dve.Fori(2, FIRST + 2) as t:
                ch.loop(t - 2, first, 1)
                bias1(t)
                x_evac(t + 1)
                shared_out(t - 2, tile_of(h, t - 2))
                h_evac(t - 1)
            ch.leave(first, 1, FIRST)
            bias1(FIRST + 2)
            x_evac(FIRST + 3)
            ch.settled()
            bias2(FIRST)
            h_evac(FIRST + 1)
            with dve.Fori(FIRST + 3, SORTED + 2) as t:
                bias1(t)
                x_evac(t + 1)
                sorted_out(t - 2)
                h_evac(t - 1)
            dve.wait_ge(S["y_stored"], 16 * SLOT_TILES)
            for t in range(SORTED + 2, ALL_TILES + 2):
                if t < ALL_TILES:
                    bias1(t)
                if t + 1 < ALL_TILES:
                    x_evac(t + 1)
                shared_out(t - 2, h[:, t - 2 - SLOT_TILES, :])
                if t - 1 < ALL_TILES:
                    h_evac(t - 1)
                if t > SORTED + 2:
                    for n in range(2):
                        combine(2 * (t - 3 - SORTED) + n)
            for n in range(2):
                combine(TILES - 2 + n)

        @block.tensor
        def _(pe):
            t_ = nc.tensor
            pe.wait_ge(S["c_loaded"], 16 * C_LOADS)
            pe.wait_ge(S["pn_ready"], ROUNDS)
            for k in range(KP):
                if k >= 2:
                    pe.wait_ge(S["pn_put"], k - 1)
                for i in range(ROUNDS):
                    last = t_.transpose(ps[:, 7 if k % 2 == 0 else 0, P * i:P * (i + 1)],
                                        pn[:, i, P * k:P * (k + 1)], ident[:])
                last.then_inc(S["pn_tr"], 1)
            pe.wait_ge(S["w_put"], KP)
            pe.wait_ge(S["pn_put"], KP)
            for i in range(ROUNDS):
                for k in range(KP):
                    last = t_.matmul(ps[:, 1 + i, 0:D], pn_t[:, k, i, :], tw_t[:, k, :], start=k == 0, stop=k == KP - 1)
                last.then_inc(S["tok_mm"], 1)
            pe.wait_ge(S["tok_done"], 1)

            def transpose_xn(i, n):
                if n < 2:
                    reach(pe, S["v_put"], 2 * i - 1 + n)
                else:
                    pe.wait_ge(S["xn_put"], xn_puts(i, 1))
                pe.wait_ge(S["xn_ready"], R_TILES * i + n + 1)
                for k in range(KD):
                    last = t_.transpose(ps[:, SIDE_BANK["T"][n], P * k:P * (k + 1)], xn[:, n, P * k:P * (k + 1)],
                                        ident[:])
                last.then_inc(S["xn_tr"], 1)

            def project(i, n):
                w, r = divmod(n, 2)
                pe.wait_ge(S["xn_put"], xn_puts(i, 3))
                if w == 0:
                    reach(pe, S["h_new"], R_TILES * (i - 2) + 2 + r)
                else:
                    pe.wait_ge(S["q_put"], 4 * i + 2 * (r + 1))
                for k in range(KD):
                    last = t_.matmul(ps[:, SIDE_BANK["QK"[w]][r], 0:R_TOK], w_t[:, w, k, P * r:P * (r + 1)],
                                     xn_t[:, k, :, 0:SEQ], start=k == 0, stop=k == KD - 1)
                last.then_inc(S["proj"], 1)

            def make_values(i, n):
                if i < 2:
                    pe.wait_ge(S["k_put"], 2 * i + n + 1)
                elif n == 0:
                    pe.wait_ge(S["xf_put"], R_TILES * (i - 1))
                else:
                    pe.wait_ge(S["rt_read"], i - 1)
                for b in range(2):
                    pair = xn_t[:, :, 2 * (2 * n + b):2 * (2 * n + b) + 2, :].rearrange("p k b t -> p k (b t)")
                    for k in range(KD):
                        last = t_.matmul(ps[:, SIDE_BANK["V"][n], D * b:D * (b + 1)], pair[:, k, :], w_t[:, 2, k, :],
                                         start=k == 0, stop=k == KD - 1)
                last.then_inc(S["v_mm"], 1)

            def output(i, n):
                if n == 2:
                    pe.wait_ge(S["h_new"], R_TILES * i + 1)
                elif i + 2 < ROUNDS:
                    pe.wait_ge(S["xn_put"], xn_puts(i + 2, 2 + n))
                elif i + 1 < ROUNDS:
                    pe.wait_ge(S["v_put"], 2 * (i + 1) + 2)
                elif n == 0:
                    pe.wait_ge(S["rt_read"], i)
                else:
                    pe.wait_ge(S["xf_put"], R_TILES * i)
                pe.wait_ge(S["o_put"], 8 * (i + 1))
                for k in range(KD):
                    last = t_.matmul(ps[:, SIDE_BANK["W"][n], 0:D], o_t[:, k, n, :], w_t[:, 3, k, :],
                                     start=k == 0, stop=k == KD - 1)
                last.then_inc(S["wo_mm"], 1)

            def transpose_xf(i, n):
                if i + 2 < ROUNDS and n < 2:
                    pe.wait_ge(S["k_put"], 2 * (i + 2) + n + 1)
                elif n == 2:
                    pe.wait_ge(S["xf_put"], R_TILES * i + 1)
                pe.wait_ge(S["xf_ready"], R_TILES * i + n + 1)
                for k in range(KD):
                    last = t_.transpose(ps[:, SIDE_BANK["X"][n], P * k:P * (k + 1)], xf_s[:, n, P * k:P * (k + 1)],
                                        ident[:])
                last.then_inc(S["xf_tr"], 1)

            def route(i):
                pe.wait_ge(S["xf_put"], R_TILES * (i + 1))
                for n in range(R_TILES):
                    for k in range(KD):
                        last = t_.matmul(ps[:, SIDE_BANK["R"][0], 8 * n:8 * n + 8], xf_t[:, n, k, :], rw[:, k, :],
                                         start=k == 0, stop=k == KD - 1)
                last.then_inc(S["rt_mm"], 1)

            def scores(i, u):
                g, r = divmod(u, 4)
                if u == 0:
                    pe.wait_ge(S["q_put"], 4 * (i + 1))
                    pe.wait_ge(S["k_put"], 2 * (i + 1))
                reach(pe, S["logits"], UNITS * i + u - 1)
                for b in range(4):
                    for k in range(KD):
                        c, at_b = SEQ * (4 * g + b), SEQ * block_of(b, k)
                        last = t_.matmul(ps[0:2 * SEQ, u % 2, at_b:at_b + SEQ],
                                         qx[32 * r:32 * (r + 1), i % 2, k, 4 * g + b].rearrange("p a q -> p (a q)"),
                                         k_t[32 * r:32 * (r + 1), i % 2, k, c:c + SEQ], start=True, stop=True)
                last.then_inc(S["scores"], 1)

            def block_of(b, k):
                return 4 * (b // 2) + 2 * k + b % 2

            def transpose_probs(n):
                if n < 0:
                    return
                b2 = n % 2
                pe.wait_ge(S["probs"], n + 1)
                reach(pe, S["pt_put"], n - 1)
                for c in range(4):
                    last = t_.transpose(ps[0:KPAD + SEQ, 2 + b2, 2 * SEQ * c:2 * SEQ * (c + 1)],
                                        pr[:, b2, 2 * c:2 * c + 2, :].rearrange("p n k -> p (n k)")
                                        [:, 0:KPAD + SEQ], ident[0:2 * SEQ, 0:2 * SEQ])
                last.then_inc(S["pr_tr"], 1)

            def attend(n):
                if n < 0:
                    return
                i, u = divmod(n, UNITS)
                g, r = divmod(u, 4)
                pe.wait_ge(S["pt_put"], UNITS * i + u + 1)
                if u == 0:
                    pe.wait_ge(S["v_put"], 2 * (i + 1))
                if r == 0:
                    reach(pe, S["o_put"], 8 * i + 4 * g)
                for b in range(4):
                    for k in range(KD):
                        keys, c = slice(KPAD * (b % 2), KPAD * (b % 2) + SEQ), 2 * (b // 2) + k
                        at_b = 256 * (b // 2) + 2 * SEQ * k
                        last = t_.matmul(ps[32 * r:32 * (r + 1), 4 + b % 2, at_b:at_b + 2 * SEQ],
                                         v[keys, i % 2, 2 * g + b // 2, P * k + 32 * r:P * k + 32 * (r + 1)],
                                         p_t[keys, u % 2, 2 * SEQ * c:2 * SEQ * (c + 1)], start=True, stop=True)
                last.then_inc(S["av"], 1)

            for n in range(R_TILES):
                transpose_xn(0, n)
            for n in range(4):
                project(0, n)
            scores(0, 0)
            for i in range(ROUNDS):
                before, after = i > 0, i + 1 < ROUNDS
                for u in range(UNITS):
                    n = UNITS * i + u
                    if u + 1 < UNITS:
                        scores(i, u + 1)
                    if after and u == 3:
                        transpose_xn(i + 1, 2)
                    if before and u == 4:
                        output(i - 1, 1)
                    if after and u == 5:
                        project(i + 1, 1)
                    if after and u == 6:
                        project(i + 1, 2)
                    if before and u == 7:
                        transpose_xf(i - 1, 0)
                    transpose_probs(n - 1)
                    attend(n - 2)
                    if u == 1:
                        make_values(i, 0)
                        make_values(i, 1)
                    if after and u == 2:
                        transpose_xn(i + 1, 0)
                        transpose_xn(i + 1, 1)
                    if before and u == 3:
                        output(i - 1, 0)
                    if before and u == 4:
                        output(i - 1, 2)
                    if after and u == 4:
                        project(i + 1, 0)
                    if after and u == 6:
                        project(i + 1, 3)
                if after:
                    scores(i + 1, 0)
                if before:
                    transpose_xf(i - 1, 1)
                    transpose_xf(i - 1, 2)
                    route(i - 1)
            transpose_probs(UNITS * ROUNDS - 1)
            attend(UNITS * ROUNDS - 2)
            attend(UNITS * ROUNDS - 1)
            for n in range(R_TILES):
                output(ROUNDS - 1, n)
            for n in range(R_TILES):
                transpose_xf(ROUNDS - 1, n)
            route(ROUNDS - 1)

            pe.wait_ge(S["cnt_ready"], TOP * ROUNDS + 1)
            pe.wait_ge(S["ones_set"], 3)
            last = t_.matmul(ps[:, 6, 0:TILES * EXPERTS], tri[:], cnt[:].rearrange("p t e -> p (t e)"),
                             start=True, stop=False)
            for j in range(TILES - 1):
                last = t_.matmul(ps[:, 6, EXPERTS * (j + 1):EXPERTS * TILES].rearrange("p (t e) -> p t e", e=EXPERTS),
                                 ones[:], cnt[:, j:j + 1, :].broadcast_to([P, TILES - 1 - j, EXPERTS]),
                                 start=False, stop=j == TILES - 2)
            for j in range(TILES):
                last = t_.matmul(ps[:, 7, 0:EXPERTS], ones[:], cnt[:, j, :], start=j == 0, stop=j == TILES - 1)
            last.then_inc(S["rank_mm"], 1)

            pe.wait_ge(S["slots_ready"], 2)

            def x_transpose(t, first=False):
                pe.wait_ge(S["xs_loaded"], 16 * (t + 1))
                if not first:
                    pe.wait_ge(S["x_put"], t)
                for k in range(KD):
                    last = t_.transpose(ps[:, 5, P * k:P * (k + 1)], xs[:, P * k:P * (k + 1)], ident[:])
                last.then_inc(S["x_tr"], 1)

            def slot_of(t):
                return pe.value_load(at[0:1, bass.ds(t, 1)], min_val=0, max_val=RING - 1)

            def in_parts(dst, hi, lo, w, chunks):
                for k in range(chunks):
                    w_hi, w_lo = w(k, 0), w(k, SPLIT)
                    for c, (x_part, w_part) in enumerate(((hi, w_lo), (lo, w_hi), (hi, w_hi))):
                        ins = t_.matmul(dst, x_part[:, k, :], w_part, start=(k, c) == (0, 0),
                                        stop=(k, c) == (chunks - 1, 2))
                return ins

            def weights(s_, w_at, n):
                return ring[:, bass.ds(s_, 1), w_at:w_at + n].rearrange("p o f -> p (o f)")

            def need_of(t):
                return pe.value_load(need[0:1, bass.ds(t, 1)], min_val=1, max_val=ORDERS)

            def layer1(t, n_w, s_):
                pe.wait_ge(S["w1_ready"], n_w)
                pe.wait_ge(S["x_put"], t + 1)
                pe.wait_ge(S["hp_ready"], 2 * t)
                for n in range(2):
                    in_parts(ps[:, n, :], x_hi, x_lo,
                             lambda k, low: weights(s_, W1_AT + FF * k + 512 * n + low, 512), KD)\
                        .then_inc(S["l1"], 1)

            def h_transpose(t):
                pe.wait_ge(S["ht_put"], 2 * t)
                for n in range(2):
                    pe.wait_ge(S["gelu"], 2 * t + n + 1)
                    for k in range(4):
                        c = P * (4 * n + k)
                        last = t_.transpose(ps[:, 2 + n, P * k:P * (k + 1)], hg[:, c:c + P], ident[:])
                    last.then_inc(S["h_tr"], 1)

            def layer2(t):
                n_w = need_of(t)
                s_ = slot_of(t)
                pe.wait_ge(S["w2_ready"], n_w)
                pe.wait_ge(S["ht_put"], 2 * t + 2)
                pe.wait_ge(S["y_ready"], t)
                in_parts(ps[:, 4, 0:D], h_hi, h_lo, lambda k, low: weights(s_, W2_AT + D * k + low, D), KF)\
                    .then_inc(S["l2"], 1)

            x_transpose(0, first=True)
            layer1(0, need_of(0), slot_of(0))
            x_transpose(1)
            layer1(1, need_of(1), slot_of(1))
            x_transpose(2)
            h_transpose(0)
            with pe.Fori(0, (ALL_TILES - 3) // 4) as turn:
                first_t = 4 * turn + 2
                now = need_of(first_t), slot_of(first_t)
                for c in range(4):
                    t = first_t + c
                    layer1(t, *now)
                    x_transpose(t + 1)
                    layer2(t - 2)
                    if c < 3:
                        now = need_of(t + 1), slot_of(t + 1)
                    h_transpose(t - 1)
            t = ALL_TILES - 1
            layer1(t, need_of(t), slot_of(t))
            layer2(t - 2)
            h_transpose(t - 1)
            layer2(t - 1)
            h_transpose(t)
            layer2(t)


_NAMES = {"txt": "txt", "ln2_w": "L0_tok_ln2_w", "bo": "L0_attn_bo",
          "shared_w1": "L0_ffn_shared_w1", "shared_b1": "L0_ffn_shared_b1", "shared_w2": "L0_ffn_shared_w2",
          "shared_b2": "L0_ffn_shared_b2", "rw": "L0_ffn_router_w", "rb": "L0_ffn_router_b",
          "exp_w1": "L0_ffn_exp_w1", "exp_b1": "L0_ffn_exp_b1", "exp_w2": "L0_ffn_exp_w2", "exp_b2": "L0_ffn_exp_b2"}


def constants():
    f = np.float32
    q, k = np.arange(SEQ)[:, None], np.arange(SEQ)[None, :]
    times = np.log(SEQ - q).astype(f)
    bias = np.where(k < q, f(0), np.where(k == q, times, f(-1e30))).astype(f)
    odd = ((np.arange(P) // HS) % 2).astype(f)
    parity = np.stack([1 - odd, odd, (1 - odd) * f(HS ** -0.5), odd * f(HS ** -0.5)], 1).astype(f)
    small = np.zeros((P, 64), f)
    small[:, 0:TILES] = P * np.arange(TILES)
    small[:, 12:12 + SLOT_TILES] = np.arange(SLOT_TILES)
    small[:, 43:43 + EXPERTS] = np.arange(EXPERTS)
    small[:, 51:50 + EXPERTS] = (-1.0) ** np.arange(EXPERTS - 1)
    omega = np.arange(D // 4, dtype=f) / f(D // 4 - 1)
    omega = (f(1) / np.power(f(10000.0), omega)).astype(f)
    yy, xx = np.meshgrid(np.arange(GRID, dtype=f), np.arange(GRID, dtype=f), indexing="ij")
    ya, xa = yy.reshape(-1)[:, None] * omega, xx.reshape(-1)[:, None] * omega
    pe = np.concatenate([np.sin(xa), np.cos(xa), np.sin(ya), np.cos(ya)], 1).astype(f)
    return {"c_ident": np.eye(P, dtype=f), "c_bias": np.tile(bias, (2, 1)), "c_parity": parity, "c_small": small,
            "c_pos": np.tile(pe, (P // IMG_TOK, 1)),
            "c_tri": (np.arange(P)[:, None] < np.arange(P)[None, :]).astype(f)}


def laid_out(inputs):
    x = np.asarray(inputs["x"]).reshape(IMAGES, CHANNELS, GRID, PATCH, GRID, PATCH)
    turned = {"tok_w": "L0_tok_W", "wq": "L0_attn_Wq", "wk": "L0_attn_Wk", "wv": "L0_attn_Wv", "wo": "L0_attn_Wo"}
    vectors = ("L0_tok_ln1_w", "L0_attn_bq", "L0_attn_bk", "L0_attn_bv")
    return {"patches": np.ascontiguousarray(x.transpose(0, 2, 4, 1, 3, 5)).reshape(IMAGES * IMG_TOK, PD),
            "vcols": np.ascontiguousarray(
                np.concatenate([np.asarray(inputs[n]).reshape(-1, P) for n in vectors], 0).T),
            **{k: np.ascontiguousarray(np.asarray(inputs[n]).T) for k, n in turned.items()}}


def build(nc, inputs, **kw):
    arrays, aps = {}, {}
    given = {k: np.ascontiguousarray(inputs[v]) for k, v in _NAMES.items()}
    for name, arr in {**given, **laid_out(inputs), **constants()}.items():
        arrays[f"in_{name}"] = arr
        aps[name] = nc.dram_tensor(f"in_{name}", arr.shape, mybir.dt.from_np(arr.dtype), kind="ExternalInput").ap()
    out = nc.dram_tensor("out_0", (IMAGES, SEQ, D), F32, kind="ExternalOutput").ap()
    program(nc, aps, out, **kw)
    return arrays


def kernel(**inputs):
    import concourse.bacc as bacc
    from concourse.bass_utils import run_bass_kernel_spmd

    nc = bacc.Bacc("TRN2", target_bir_lowering=False, num_devices=1)
    arrays = build(nc, inputs)
    r = run_bass_kernel_spmd(nc, [arrays], core_ids=[0])
    return r.results[0]["out_0"]
```
